# Optimizing a Trainium2 kernel written in Bass

```python
import numpy as np
import jax
import jax.numpy as jnp

def _softmax(x, axis=-1):
    return jax.nn.softmax(x, axis=axis)

def _gelu(x):
    return jax.nn.gelu(x, approximate=True)

def _silu(x):
    return jax.nn.silu(x)

def _sigmoid(x):
    return jax.nn.sigmoid(x)

def _layernorm(x, axis=-1, eps=1e-05):
    m = jnp.mean(x, axis=axis, keepdims=True)
    v = jnp.var(x, axis=axis, keepdims=True)
    return (x - m) / jnp.sqrt(v + eps)

def _scatter_add(tgt, idx, src, axis=0):
    return tgt.at[idx].add(src)

def _segment_sum(src, seg, n):
    return jax.ops.segment_sum(src, seg, n)
kernel_name = 'mk_recurrent_d2_jaxref_r8_ff90d6'

def setup_inputs(seed: int=0):
    np.random.seed(seed)
    _w = jnp.asarray

    def _L0_attn_setup():
        import jax, jax.numpy as jnp
        import numpy as np
        B, T, D, H = (8, 512, 128, 8)

        def _block_linear(x, w, b):
            Bx, Tx, Dx = x.shape
            h, bw = (w.shape[0], w.shape[1])
            xb = x.reshape(Bx, Tx, h, bw)
            y = jnp.einsum('bthi,hij->bthj', xb, w) + b
            return y.reshape(Bx, Tx, Dx)

        def _rglru(x, a_param, ig_w, ig_b, ag_w, ag_b, sqrt_fn):
            gate_x = jax.nn.sigmoid(_block_linear(x, ig_w, ig_b))
            gate_a = jax.nn.sigmoid(_block_linear(x, ag_w, ag_b))
            log_a = -8.0 * gate_a * jax.nn.softplus(a_param)
            a = jnp.exp(log_a)
            a2 = jnp.exp(2.0 * log_a)
            multiplier = sqrt_fn(jnp.maximum(1.0 - a2, 1e-07))
            normed_x = x * gate_x * multiplier
            p = jnp.cumprod(a, axis=1)
            p_prefix = jnp.concatenate([jnp.ones_like(p[:, :1]), p[:, :-1]], axis=1)
            p_prefix = jnp.maximum(p_prefix, 1e-07)
            S = jnp.cumsum(normed_x / p_prefix, axis=1)
            h = p_prefix * S
            return (h, h[:, -1, :])

        def _reference_tuple_inner(x, segment_pos, a_param, ig_w, ig_b, ag_w, ag_b):
            y, last_h = _rglru(x, a_param, ig_w, ig_b, ag_w, ag_b, jnp.sqrt)
            return (y, last_h)
        key = jax.random.key(seed)
        k0, k1, k2, k3 = jax.random.split(key, 4)
        bw = D // H
        std = (1.0 / bw) ** 0.5
        x = jax.random.normal(k0, (B, T, D), dtype=jnp.float32)
        segment_pos = jnp.tile(jnp.arange(T, dtype=jnp.int32)[None, :], (B, 1))
        ig_w = jax.random.normal(k1, (H, bw, bw), dtype=jnp.float32) * std
        ig_b = jnp.zeros((H, bw), dtype=jnp.float32)
        ag_w = jax.random.normal(k2, (H, bw, bw), dtype=jnp.float32) * std
        ag_b = jnp.zeros((H, bw), dtype=jnp.float32)
        eps = 1e-08
        u = jax.random.uniform(k3, (D,), minval=0.9 ** 2 + eps, maxval=0.999 ** 2 + eps)
        a_param = jnp.log(jnp.exp(-0.5 * jnp.log(u)) - 1.0).astype(jnp.float32)
        return dict(x=x, segment_pos=segment_pos, a_param=a_param, ig_w=ig_w, ig_b=ig_b, ag_w=ag_w, ag_b=ag_b)
    _L0_attn_in = _L0_attn_setup()

    def _L0_ffn_setup():
        import jax, jax.numpy as jnp
        import numpy as np
        TOP_K = 2
        EPS = 1e-20
        key = jax.random.key(seed)
        ks = jax.random.split(key, 8)
        B, S, H, E, D = (4, 256, 128, 8, 256)
        s = 0.02
        return {'x': jax.random.normal(ks[0], (B, S, H), dtype=jnp.float32), 'Wr': jax.random.normal(ks[1], (H, E), dtype=jnp.float32) * s, 'Wg': jax.random.normal(ks[2], (E, H, D), dtype=jnp.float32) * s, 'Wu': jax.random.normal(ks[3], (E, H, D), dtype=jnp.float32) * s, 'Wd': jax.random.normal(ks[4], (E, D, H), dtype=jnp.float32) * s, 'Sg': jax.random.normal(ks[5], (H, D), dtype=jnp.float32) * s, 'Su': jax.random.normal(ks[6], (H, D), dtype=jnp.float32) * s, 'Sd': jax.random.normal(ks[7], (D, H), dtype=jnp.float32) * s}
    _L0_ffn_in = _L0_ffn_setup()

    def _L1_attn_setup():
        import jax, jax.numpy as jnp
        import numpy as np
        THETA = 10000.0

        def rope_rotate(x):
            T, C = (x.shape[-2], x.shape[-1])
            inv_freq = 1.0 / THETA ** (jnp.arange(0, C, 2, dtype=jnp.float32) / C)
            freqs = jnp.arange(T, dtype=jnp.float32)[:, None] * inv_freq[None, :]
            freqs = jnp.repeat(freqs, 2, axis=-1)
            cos, sin = (jnp.cos(freqs), jnp.sin(freqs))
            xp = x.reshape(x.shape[:-1] + (C // 2, 2))
            x_rot = jnp.stack((-xp[..., 1], xp[..., 0]), axis=-1).reshape(x.shape)
            return x * cos + x_rot * sin
        key = jax.random.key(seed)
        ks = jax.random.split(key, 5)
        B, T, C = (4, 256, 128)
        s = 1.0 / np.sqrt(C)
        return {'x': jax.random.normal(ks[0], (B, T, C), jnp.float32), 'Wq': jax.random.normal(ks[1], (C, C), jnp.float32) * s, 'bq': jnp.zeros((C,), jnp.float32), 'Wk': jax.random.normal(ks[2], (C, C), jnp.float32) * s, 'bk': jnp.zeros((C,), jnp.float32), 'Wv': jax.random.normal(ks[3], (C, C), jnp.float32) * s, 'bv': jnp.zeros((C,), jnp.float32), 'Wo': jax.random.normal(ks[4], (C, C), jnp.float32) * s, 'bo': jnp.zeros((C,), jnp.float32)}
    _L1_attn_in = _L1_attn_setup()

    def _L1_ffn_setup():
        import jax, jax.numpy as jnp
        import numpy as np
        BS, SLEN, DIM = (1, 256, 128)
        NUM_EXPERTS, TOP_K = (8, 2)
        HID = 176

        def _masked_grouped_mm(x, w, onehot):
            g = jnp.einsum('tk,gnk->tgn', x, w, preferred_element_type=jnp.float32)
            return jnp.einsum('tgn,tg->tn', g, onehot)

        def moe_forward(x, gate_w, expert_bias, w_up, w_down, shared_w_up, shared_w_down):
            bs, slen, dim = x.shape
            xf = x.reshape(-1, dim)
            scores = jax.nn.sigmoid((xf @ gate_w.T).astype(jnp.float32))
            biased = scores + expert_bias
            _, sel = jax.lax.top_k(biased, TOP_K)
            top_scores = jnp.take_along_axis(scores, sel, axis=-1)
            flat_sel = sel.reshape(-1)
            counts = jnp.bincount(flat_sel, length=NUM_EXPERTS)
            order = jnp.argsort(flat_sel, stable=True)
            scores_sorted = top_scores.reshape(-1)[order]
            token_ids = order // TOP_K
            routed_in = (xf[token_ids] * scores_sorted[:, None]).astype(x.dtype)
            seg = jnp.repeat(jnp.arange(NUM_EXPERTS), counts, total_repeat_length=flat_sel.shape[0])
            onehot = jax.nn.one_hot(seg, NUM_EXPERTS, dtype=jnp.float32)
            h = _masked_grouped_mm(routed_in.astype(jnp.bfloat16), w_up.astype(jnp.bfloat16), onehot)
            h = jnp.square(jax.nn.relu(h.astype(jnp.bfloat16)))
            routed_out = _masked_grouped_mm(h.astype(jnp.bfloat16), w_down.astype(jnp.bfloat16), onehot)
            routed_out = routed_out.astype(jnp.bfloat16).astype(x.dtype)
            hs = jnp.square(jax.nn.relu(xf @ shared_w_up.T))
            shared_out = hs @ shared_w_down.T
            combined = jnp.zeros((flat_sel.shape[0], dim), routed_out.dtype).at[order].set(routed_out)
            out = combined.reshape(-1, TOP_K, dim).sum(axis=1) + shared_out
            return out.reshape(bs, slen, dim)
        key = jax.random.key(seed)
        k = jax.random.split(key, 6)
        s = 0.02
        return {'x': jax.random.normal(k[0], (BS, SLEN, DIM), jnp.float32), 'gate_w': jax.random.normal(k[1], (NUM_EXPERTS, DIM), jnp.float32) * s, 'expert_bias': jnp.zeros((NUM_EXPERTS,), jnp.float32), 'w_up': jax.random.normal(k[2], (NUM_EXPERTS, HID, DIM), jnp.float32) * s, 'w_down': jax.random.normal(k[3], (NUM_EXPERTS, DIM, HID), jnp.float32) * s, 'shared_w_up': jax.random.normal(k[4], (HID, DIM), jnp.float32) * s, 'shared_w_down': jax.random.normal(k[5], (DIM, HID), jnp.float32) * s}
    _L1_ffn_in = _L1_ffn_setup()
    _d = {'L0_attn_x': _L0_attn_in['x'], 'L0_attn_segment_pos': _L0_attn_in['segment_pos'], 'L0_attn_a_param': _L0_attn_in['a_param'], 'L0_attn_ig_w': _L0_attn_in['ig_w'], 'L0_attn_ig_b': _L0_attn_in['ig_b'], 'L0_attn_ag_w': _L0_attn_in['ag_w'], 'L0_attn_ag_b': _L0_attn_in['ag_b'], 'L0_ffn_Wr': _L0_ffn_in['Wr'], 'L0_ffn_Wg': _L0_ffn_in['Wg'], 'L0_ffn_Wu': _L0_ffn_in['Wu'], 'L0_ffn_Wd': _L0_ffn_in['Wd'], 'L0_ffn_Sg': _L0_ffn_in['Sg'], 'L0_ffn_Su': _L0_ffn_in['Su'], 'L0_ffn_Sd': _L0_ffn_in['Sd'], 'L1_attn_Wq': _L1_attn_in['Wq'], 'L1_attn_bq': _L1_attn_in['bq'], 'L1_attn_Wk': _L1_attn_in['Wk'], 'L1_attn_bk': _L1_attn_in['bk'], 'L1_attn_Wv': _L1_attn_in['Wv'], 'L1_attn_bv': _L1_attn_in['bv'], 'L1_attn_Wo': _L1_attn_in['Wo'], 'L1_attn_bo': _L1_attn_in['bo'], 'L1_ffn_gate_w': _L1_ffn_in['gate_w'], 'L1_ffn_expert_bias': _L1_ffn_in['expert_bias'], 'L1_ffn_w_up': _L1_ffn_in['w_up'], 'L1_ffn_w_down': _L1_ffn_in['w_down'], 'L1_ffn_shared_w_up': _L1_ffn_in['shared_w_up'], 'L1_ffn_shared_w_down': _L1_ffn_in['shared_w_down']}
    _x0 = _d['L0_attn_x']
    _d['L0_attn_x'] = jax.random.normal(jax.random.fold_in(jax.random.key(seed), 1), (16, 512, 128), dtype=_x0.dtype)
    del _x0
    return _d

def reference(L0_attn_x, L0_attn_segment_pos, L0_attn_a_param, L0_attn_ig_w, L0_attn_ig_b, L0_attn_ag_w, L0_attn_ag_b, L0_ffn_Wr, L0_ffn_Wg, L0_ffn_Wu, L0_ffn_Wd, L0_ffn_Sg, L0_ffn_Su, L0_ffn_Sd, L1_attn_Wq, L1_attn_bq, L1_attn_Wk, L1_attn_bk, L1_attn_Wv, L1_attn_bv, L1_attn_Wo, L1_attn_bo, L1_ffn_gate_w, L1_ffn_expert_bias, L1_ffn_w_up, L1_ffn_w_down, L1_ffn_shared_w_up, L1_ffn_shared_w_down):

    def _L0_attn_ref(x, segment_pos, a_param, ig_w, ig_b, ag_w, ag_b):
        import jax, jax.numpy as jnp
        import numpy as np
        B, T, D, H = (8, 512, 128, 8)

        def _block_linear(x, w, b):
            Bx, Tx, Dx = x.shape
            h, bw = (w.shape[0], w.shape[1])
            xb = x.reshape(Bx, Tx, h, bw)
            y = jnp.einsum('bthi,hij->bthj', xb, w) + b
            return y.reshape(Bx, Tx, Dx)

        def _rglru(x, a_param, ig_w, ig_b, ag_w, ag_b, sqrt_fn):
            gate_x = jax.nn.sigmoid(_block_linear(x, ig_w, ig_b))
            gate_a = jax.nn.sigmoid(_block_linear(x, ag_w, ag_b))
            log_a = -8.0 * gate_a * jax.nn.softplus(a_param)
            a = jnp.exp(log_a)
            a2 = jnp.exp(2.0 * log_a)
            multiplier = sqrt_fn(jnp.maximum(1.0 - a2, 1e-07))
            normed_x = x * gate_x * multiplier
            p = jnp.cumprod(a, axis=1)
            p_prefix = jnp.concatenate([jnp.ones_like(p[:, :1]), p[:, :-1]], axis=1)
            p_prefix = jnp.maximum(p_prefix, 1e-07)
            S = jnp.cumsum(normed_x / p_prefix, axis=1)
            h = p_prefix * S
            return (h, h[:, -1, :])

        def _reference_tuple_inner(x, segment_pos, a_param, ig_w, ig_b, ag_w, ag_b):
            y, last_h = _rglru(x, a_param, ig_w, ig_b, ag_w, ag_b, jnp.sqrt)
            return (y, last_h)
        return _reference_tuple_inner(x, segment_pos, a_param, ig_w, ig_b, ag_w, ag_b)[0]

    def _L0_ffn_ref(x, Wr, Wg, Wu, Wd, Sg, Su, Sd):
        import jax, jax.numpy as jnp
        import numpy as np
        TOP_K = 2
        EPS = 1e-20
        B, S, H = x.shape
        T = B * S
        xt = x.reshape(T, H)
        scores = jax.nn.softmax(xt @ Wr, axis=-1)
        topk_w, topk_idx = jax.lax.top_k(scores, TOP_K)
        topk_w = topk_w / (topk_w.sum(axis=-1, keepdims=True) + EPS)
        g = jax.nn.silu(jnp.einsum('th,ehd->etd', xt, Wg))
        u = jnp.einsum('th,ehd->etd', xt, Wu)
        out_all = jnp.einsum('etd,edh->eth', g * u, Wd)
        tok = jnp.arange(T)[:, None]
        gathered = out_all[topk_idx, tok, :]
        out = jnp.sum(gathered * topk_w[..., None], axis=1).reshape(B, S, H)
        shared = jax.nn.silu(x @ Sg) * (x @ Su) @ Sd
        return out + shared

    def _L1_attn_ref(x, Wq, bq, Wk, bk, Wv, bv, Wo, bo):
        import jax, jax.numpy as jnp
        import numpy as np
        THETA = 10000.0

        def rope_rotate(x):
            T, C = (x.shape[-2], x.shape[-1])
            inv_freq = 1.0 / THETA ** (jnp.arange(0, C, 2, dtype=jnp.float32) / C)
            freqs = jnp.arange(T, dtype=jnp.float32)[:, None] * inv_freq[None, :]
            freqs = jnp.repeat(freqs, 2, axis=-1)
            cos, sin = (jnp.cos(freqs), jnp.sin(freqs))
            xp = x.reshape(x.shape[:-1] + (C // 2, 2))
            x_rot = jnp.stack((-xp[..., 1], xp[..., 0]), axis=-1).reshape(x.shape)
            return x * cos + x_rot * sin
        B, T, C = x.shape
        Q = rope_rotate(x @ Wq + bq)
        K = rope_rotate(x @ Wk + bk)
        V = x @ Wv + bv
        A = jnp.einsum('btc,bsc->bts', Q, K) / jnp.sqrt(jnp.float32(C))
        causal = jnp.tril(jnp.ones((T, T), dtype=bool))
        A = jnp.where(causal, A, -jnp.inf)
        P = jax.nn.softmax(A, axis=-1)
        out = jnp.einsum('bts,bsc->btc', P, V)
        return out @ Wo + bo

    def _L1_ffn_ref(x, gate_w, expert_bias, w_up, w_down, shared_w_up, shared_w_down):
        import jax, jax.numpy as jnp
        import numpy as np
        BS, SLEN, DIM = (1, 256, 128)
        NUM_EXPERTS, TOP_K = (8, 2)
        HID = 176

        def _masked_grouped_mm(x, w, onehot):
            g = jnp.einsum('tk,gnk->tgn', x, w, preferred_element_type=jnp.float32)
            return jnp.einsum('tgn,tg->tn', g, onehot)

        def moe_forward(x, gate_w, expert_bias, w_up, w_down, shared_w_up, shared_w_down):
            bs, slen, dim = x.shape
            xf = x.reshape(-1, dim)
            scores = jax.nn.sigmoid((xf @ gate_w.T).astype(jnp.float32))
            biased = scores + expert_bias
            _, sel = jax.lax.top_k(biased, TOP_K)
            top_scores = jnp.take_along_axis(scores, sel, axis=-1)
            flat_sel = sel.reshape(-1)
            counts = jnp.bincount(flat_sel, length=NUM_EXPERTS)
            order = jnp.argsort(flat_sel, stable=True)
            scores_sorted = top_scores.reshape(-1)[order]
            token_ids = order // TOP_K
            routed_in = (xf[token_ids] * scores_sorted[:, None]).astype(x.dtype)
            seg = jnp.repeat(jnp.arange(NUM_EXPERTS), counts, total_repeat_length=flat_sel.shape[0])
            onehot = jax.nn.one_hot(seg, NUM_EXPERTS, dtype=jnp.float32)
            h = _masked_grouped_mm(routed_in.astype(jnp.bfloat16), w_up.astype(jnp.bfloat16), onehot)
            h = jnp.square(jax.nn.relu(h.astype(jnp.bfloat16)))
            routed_out = _masked_grouped_mm(h.astype(jnp.bfloat16), w_down.astype(jnp.bfloat16), onehot)
            routed_out = routed_out.astype(jnp.bfloat16).astype(x.dtype)
            hs = jnp.square(jax.nn.relu(xf @ shared_w_up.T))
            shared_out = hs @ shared_w_down.T
            combined = jnp.zeros((flat_sel.shape[0], dim), routed_out.dtype).at[order].set(routed_out)
            out = combined.reshape(-1, TOP_K, dim).sum(axis=1) + shared_out
            return out.reshape(bs, slen, dim)
        return moe_forward(x, gate_w, expert_bias, w_up, w_down, shared_w_up, shared_w_down)
    x = L0_attn_x
    xn = _layernorm(x, axis=-1)
    s = _L0_attn_ref(xn, L0_attn_segment_pos, L0_attn_a_param, L0_attn_ig_w, L0_attn_ig_b, L0_attn_ag_w, L0_attn_ag_b)
    g = _silu(_L0_ffn_ref(xn, L0_ffn_Wr, L0_ffn_Wg, L0_ffn_Wu, L0_ffn_Wd, L0_ffn_Sg, L0_ffn_Su, L0_ffn_Sd))
    x = x + s * g
    xn = _layernorm(x, axis=-1)
    s = _L1_attn_ref(xn, L1_attn_Wq, L1_attn_bq, L1_attn_Wk, L1_attn_bk, L1_attn_Wv, L1_attn_bv, L1_attn_Wo, L1_attn_bo)
    g = _silu(_L1_ffn_ref(xn, L1_ffn_gate_w, L1_ffn_expert_bias, L1_ffn_w_up, L1_ffn_w_down, L1_ffn_shared_w_up, L1_ffn_shared_w_down))
    x = x + s * g
    return x

_drawn_inputs = setup_inputs


def setup_inputs(seed=0):
    import zlib

    import numpy as np

    out = dict(_drawn_inputs(seed))
    spreads = {'L0_attn_ig_b': (0.0, 2.0),
     'L0_attn_ag_b': (0.0, 2.0),
     'L1_attn_bq': (0.0, 0.8),
     'L1_attn_bk': (0.0, 0.8),
     'L1_attn_bv': (0.0, 0.8),
     'L1_attn_bo': (0.0, 2.0),
     'L1_ffn_expert_bias': (0.0, 0.8)}
    factors = {'L0_attn_a_param': 3.156,
     'L0_attn_ag_w': 3.558,
     'L0_ffn_Wr': 21.329,
     'L1_attn_Wq': 8.0,
     'L1_attn_Wk': 8.0,
     'L1_attn_Wv': 8.0,
     'L1_attn_Wo': 8.0,
     'L1_ffn_gate_w': 8.0,
     'L1_ffn_w_up': 8.0,
     'L1_ffn_w_down': 8.0,
     'L1_ffn_shared_w_up': 8.0,
     'L1_ffn_shared_w_down': 8.0}
    for name, (base, spread) in spreads.items():
        noise = np.random.default_rng([zlib.crc32(name.encode()), seed]).standard_normal(out[name].shape)
        drawn = base * np.exp(spread * noise) if base else spread * noise
        out[name] = jnp.asarray(drawn.astype(out[name].dtype))
    for name, factor in factors.items():
        out[name] = (out[name] * factor).astype(out[name].dtype)
    return out
```

```python
import concourse.bass as bass
from concourse import mybir
from contextlib import ExitStack

P = 128
NB = 16
T = 512
NT = T // P
E = 8
HID0 = 256
HID1 = 176
REM = HID1 - P
HALF = 64
NH = (E + 1) * HID0 // P
EPS = 1e-5
FLOOR = 1e-7
LN_FLOOR = -16.11809565095832
MASKED = -1e37

W_ROUTE0 = 0
W_ROUTE1 = W_ROUTE0 + E
W_IG = W_ROUTE1 + E
W_AG = W_IG + P
W_GU = W_AG + P
W_D = W_GU + (E + 1) * 2 * HID0
W_Q = W_D + (E + 1) * HID0
W_QS, W_K, W_KS, W_V, W_O = (W_Q + P * n for n in range(1, 6))
W_SU = W_O + P
W_SD = W_SU + 2 * P
W_ALL = W_SD + 2 * P
W_CHUNKS = 16
W_CHUNK = W_ALL // W_CHUNKS
assert W_CHUNK * W_CHUNKS == W_ALL
V_U = 0
V_UR = V_U + E * P
V_D = V_UR + E // 2 * P
V_DR = V_D + E * P
V_ALL = V_DR + E // 2 * P
V_CHUNK = 2 * T
V_CHUNKS = V_ALL // V_CHUNK
C_IG, C_AG, C_A, C_Q, C_QS, C_K, C_KS, C_V, C_O, C_N = range(10)

SCHEDULE = {
    (0, 0): ["b_silu"],
    (1, 2): ["b_tsg"],
    (2, 0): ["r_up"], (2, 2): ["a_load"],
    (3, 0): ["r_scan"], (3, 2): ["m_g4"],
    (4, 0): ["b_xt"],
    (4, 2): ["a_norm"],
    (5, 0): ["b_q"], (5, 1): ["b_qs"], (5, 2): ["b_k", "m_g5"],
    (6, 0): ["b_ks"], (6, 1): ["b_route", "b_qsum"], (6, 2): ["b_v"],
    (7, 0): ["b_ksum", "a_xt"], (7, 1): ["b_su0"], (7, 2): ["m_g6"],
    (8, 0): ["b_su1", "a_logits"], (8, 1): ["b_s02"], (8, 2): ["b_s3"],
    (9, 0): ["b_s1"], (9, 2): ["x_exp", "b_gt", "m_g7"],
    (10, 0): ["r_fin", "b_pn"], (10, 1): ["a_gate"], (10, 2): ["b_sd", "b_g0", "b_g1", "b_g2", "b_g3"],
    (11, 0): ["b_pt0"], (11, 1): ["b_pt1"], (11, 2): ["b_pt2", "a_gt", "a_g0"],
    (12, 0): ["b_x0", "b_g4", "b_g5"], (12, 1): ["b_u0"], (12, 2): ["b_pv", "b_u1"],
    (13, 0): ["b_o", "b_ur0"], (13, 1): ["b_x1", "b_g6", "b_g7"], (13, 2): ["b_u2", "a_g1"],
    (14, 0): ["b_u3"], (14, 1): ["b_ur1", "b_x2"], (14, 2): ["b_u4"],
    (15, 0): ["b_d0", "b_u5"], (15, 1): ["b_ur2", "b_x3"], (15, 2): ["b_u6", "a_g2"],
    (16, 0): ["b_d1", "b_u7"], (16, 1): ["b_ur3"], (16, 2): ["b_d2"],
    (17, 0): ["b_d3"], (17, 1): ["b_fin"], (17, 2): ["b_out", "a_g3"],
}
RING = 4
LAG = 2


class At:

    def __init__(self, n, parity=None):
        self.n = n
        self.parity = n % 2 if parity is None else parity

    def __add__(self, k):
        return At(self.n + k, (self.parity + k) % 2)

    def batch(self, step):
        return self + {"a": 1, "m": 0, "r": 0, "x": 0, "b": -1}[step[0]]

    def has(self, stage):
        if not isinstance(self.n, int):
            return True
        return {"a": -1 <= self.n < NB - 1, "m": 0 <= self.n < NB, "r": self.n < NB, "x": True, "b": self.n > 0}[stage]


def steps(i, h, part):
    return [s for s in SCHEDULE.get((h, part), []) if i.has(s[0])]


def order(i, way_up):
    out = []
    for h in range(NH):
        for part in range(3):
            if i.has("m") and part == way_up:
                out.append(("up", h))
            out += steps(i, h, part)
    return out


class Ring:

    LEAD = ["a_xt", "a_logits", "a_gt"]

    def __init__(self, full, banks, uses, way_up=None):
        self.full, self.banks, self.uses, self.way_up = full, banks, uses, way_up
        self.read = {}
        self.length = len(self._of(At(2)))
        assert self.length % 2 == 0

    def _of(self, i):
        return [u for u in order(i, self.way_up) if (u if isinstance(u, str) else u[0]) in self.uses]

    def _until(self, n):
        users = [(u, At(-1)) for u in self.LEAD if u in self.uses]
        for k in range(n):
            users += [(u, At(k)) for u in self._of(At(k))]
        return users

    def number(self, i, user):
        if i.n == -1 if isinstance(i.n, int) else False:
            return [u for u, _ in self._until(0)].index(user), 0
        if isinstance(i.n, int):
            return len(self._until(i.n)) + self._of(i).index(user), 0
        return len(self._until(2)) - 2 * self.length + self._of(At(2)).index(user), self.length

    def bank(self, i, user):
        return self.banks[self.number(i, user)[0] % 2]

    def filled(self, i, user):
        n, per = self.number(i, user)
        return per * i.n + (n + 1) if per else n + 1

    def previous(self, i, user):
        if isinstance(i.n, int):
            n = self.number(i, user)[0]
            return (self._until(i.n + 1))[n - 2] if n >= 2 else None
        users = self._of(At(2))
        at = users.index(user) - 2
        return (users[at], i) if at >= 0 else (users[at], i + -1)


def build_layers(nc, x, weights, weights16, columns, rope, masks, rank_ties, expert_bias, out):
    F32, F32R, BF16 = mybir.dt.float32, mybir.dt.float32r, mybir.dt.bfloat16
    ALU, ACT, AX = mybir.AluOpType, mybir.ActivationFunctionType, mybir.AxisListType
    SCALE = float(P) ** -0.5

    with ExitStack() as ctx:
        def sb(name, shape, dt=F32):
            return ctx.enter_context(nc.sbuf_tensor(name, shape, dt))

        def sem(name):
            return ctx.enter_context(nc.semaphore(name))

        def bank(name):
            return ctx.enter_context(nc.psum_tensor(name, [P, T], F32))

        w_hi = sb("w_hi", [P, W_ALL], F32R)
        w_lo = sb("w_lo", [P, W_ALL], F32R)
        w16 = sb("w16", [P, V_ALL], BF16)
        cols = sb("cols", [P, C_N])
        cos_sin = sb("cos_sin", [P, 2, T])
        const = sb("const", [P, 2, P])
        ident, causal = const[:, 0, :], const[:, 1, :]
        ties = sb("ties", [P, E, E])
        bias8 = sb("bias8", [P, E])
        ln_floor = sb("ln_floor", [P, 1])
        minus_half = sb("minus_half", [P, NT])
        half_bias = sb("half_bias", [P, 2])
        decay = sb("decay", [P, 6])
        x_in = sb("x_in", [P, 2, NT, P])
        stats0 = sb("stats0", [P, NT, 6])
        mv0 = sb("mv0", [P, NT, 2])
        var0 = sb("var0", [P, NT])
        rstd0 = sb("rstd0", [P, NT])
        xn0 = sb("xn0", [P, NT, P])
        xn1 = xn0
        x0t = sb("x0t", [P, T])
        x0_hi = sb("x0_hi", [P, 2, T], F32R)
        x0_lo = sb("x0_lo", [P, 2, T], F32R)
        logit = sb("logit", [P, NT, E])
        top = sb("top", [P, NT, 4])
        score0 = sb("score0", [P, NT, E])
        beats = sb("beats", [P, NT, E, E])
        rank = sb("rank", [P, NT, E])
        gate0 = sb("gate0", [P, NT, E])
        gate0_t = sb("gate0_t", [E, T])
        gates0 = sb("gates0", [P, RING, T])
        w_stage = gates0[:].rearrange("p r t -> p (r t)")[:, 0:2 * W_CHUNK].rearrange("p (s w) -> p s w", s=2)
        silu = sb("silu", [P, 2, T])
        hid = sb("hid", [P, 3, T])
        hid_hi = sb("hid_hi", [P, 3, T], F32R)
        hid_lo = sb("hid_lo", [P, 3, T], F32R)
        tanh_x = sb("tanh_x", [P, T])
        tanh_a = sb("tanh_a", [P, T])
        log_a = tanh_a
        level = sb("level", [P, T])
        step_a = sb("step_a", [P, T])
        sq = level
        normed = tanh_x
        state = sb("state", [P, T])
        ctxt = sb("ctxt", [P, T])
        g0 = ctxt
        sg0 = g0
        x1 = sb("x1", [P, NT, P])
        stats1 = sb("stats1", [P, NT, 6])
        mv1 = sb("mv1", [P, NT, 2])
        var1 = sb("var1", [P, NT])
        rstd1 = sb("rstd1", [P, NT])
        x1t = sb("x1t", [P, T])
        x1_hi = sb("x1_hi", [P, T], F32R)
        x1_lo = sb("x1_lo", [P, T], F32R)
        rot = sb("rot", [P, 4, T])
        pt_hi = sb("pt_hi", [P, 3, T], F32R)
        pt_lo = sb("pt_lo", [P, 3, T], F32R)
        q_hi, q_lo, k_hi, k_lo = pt_hi[:, 0], pt_lo[:, 0], pt_hi[:, 1], pt_lo[:, 1]
        v_hi = sb("v_hi", [P, T], F32R)
        v_lo = sb("v_lo", [P, T], F32R)
        top1 = sb("top1", [P, 4 * NT])
        smax, nmax, ssum, rsum = (top1[:, NT * n:NT * (n + 1)] for n in range(4))
        prob = sb("prob", [P, NT * (NT + 1) // 2 * P])
        ctx_hi = sb("ctx_hi", [P, T], F32R)
        ctx_lo = sb("ctx_lo", [P, T], F32R)
        attn = sb("attn", [P, T])
        tanh1 = sb("tanh1", [P, NT, E])
        score1 = sb("score1", [P, NT, E])
        biased = sb("biased", [P, NT, E])
        beats1 = beats
        rank1 = sb("rank1", [P, NT, E])
        gate1 = sb("gate1", [P, NT, E])
        gate1_t = sb("gate1_t", [E, T])
        gates1 = sb("gates1", [P, RING, T])
        hs = sb("hs", [P, 2, T])
        hs1 = sb("hs1", [P, 2, T], F32R)
        hs_hi = [pt_hi[:, 2], hs1[:, 0]]
        hs_lo = [pt_lo[:, 2], hs1[:, 1]]
        routed_in = sb("routed_in", [P, 4, T], BF16)
        rot16 = rot[:].rearrange("p k t -> p (k t)").bitcast(BF16).rearrange("p (k t) -> p k t", k=8)
        hid16, relu16 = rot16[:, 0:6], rot16[:, 6:8]
        g1 = hs[:, 0]
        sg1 = g1
        y_out = x1

        gate0_dram = nc.dram_tensor("gate0_scratch", [2, E * T], F32).ap()
        gate1_dram = nc.dram_tensor("gate1_scratch", [2, E * T], F32).ap()

        G = Ring(sem("g_full"), [bank("g_even"), bank("g_odd")], ("up", "b_tsg", "r_up", "a_xt", "a_gt"), way_up=0)
        U = Ring(sem("u_full"), [bank("u_even"), bank("u_odd")], ("up", "r_up", "a_logits"), way_up=1)
        B_USES = ("b_xt", "b_q", "b_qs", "b_k", "b_ks", "b_route", "b_v", "b_su0", "b_su1", "b_s02", "b_s3",
                  "b_gt", "b_pt0", "b_pt1", "b_pt2", "b_pv", "b_o", "b_out",
                  *(f"b_u{e}" for e in range(E)), *(f"b_ur{e}" for e in range(E // 2)))
        Z = Ring(sem("z_full"), [bank("z_even"), bank("z_odd")], B_USES)
        y0 = bank("y0")
        y1 = bank("y1")

        w_in = [sem("w_in_even"), sem("w_in_odd")]
        w16_in = [sem("w16_in_even"), sem("w16_in_odd")]
        cols_in, rope_in, const_in, ties_in, bias8_in = (
            sem(n) for n in ("cols_in", "rope_in", "const_in", "ties_in", "bias8_in"))
        w_rounded, w_split, w16_cast, const_set, half_set = (
            sem(n) for n in ("w_rounded", "w_split", "w16_cast", "const_set", "half_set"))
        soft_dve, soft_act = sem("soft_dve"), sem("soft_act")

        counts = {}

        def signal(name, per):
            s = sem(name)
            counts[id(s)] = per
            return s

        passed_sp, passed_dve = sem("passed_sp"), sem("passed_dve")

        def upto(s, b, k):
            value = counts[id(s)] * b.n + k
            return max(value, 0) if isinstance(value, int) else value

        def emptied(ring, i, user):
            before = ring.previous(i, user)
            if before is None:
                return ring.full, 0
            last, at = before
            s, k = ring.read[last]
            return s, upto(s, at.batch("m" if isinstance(last, tuple) else last), k)

        def view(ring, i, user):
            return ring.bank(i, user)

        x_loaded = [signal("x_loaded_even", 8), signal("x_loaded_odd", 8)]
        stats0_done = signal("stats0_done", NT)
        mv0_done = signal("mv0_done", NT)
        var0_done = signal("var0_done", 1)
        rstd0_done = signal("rstd0_done", 1)
        xn0_done = signal("xn0_done", NT)
        x0t_done = signal("x0t_done", 1)
        x0_hi_done = signal("x0_hi_done", 1)
        x0_lo_done = signal("x0_lo_done", 1)
        router0 = signal("router0", 13)
        exp0_done = signal("exp0_done", 1)
        gate0_t_done = signal("gate0_t_done", 1)
        gate0_stored = signal("gate0_stored", 16)
        gates0_in = [signal(f"gates0_in_{r}", 16 * E // RING) for r in range(RING)]
        silu_done = signal("silu_done", NH)
        mul_done = signal("mul_done", NH)
        gated_done = signal("gated_done", NH - 2)
        hi_done = signal("hi_done", NH)
        lo_done = [signal(f"lo_done_{r}", NH // 3) for r in range(3)]
        down_done = signal("down_done", NH)
        tanh_done = signal("tanh_done", 2)
        log_a_done = signal("log_a_done", 1)
        level_done = signal("level_done", 2)
        step_done = signal("step_done", 2)
        a2_done = signal("a2_done", 1)
        ratio_done = signal("ratio_done", 1)
        room_done = signal("room_done", 1)
        root_done = signal("root_done", 1)
        gated_x_done = signal("gated_x_done", 1)
        normed_done = signal("normed_done", 1)
        state_done = signal("state_done", 1)
        g0_done = signal("g0_done", 1)
        sg0_done = signal("sg0_done", 1)
        x1_done = signal("x1_done", 1)
        stats1_done = signal("stats1_done", NT)
        mv1_done = signal("mv1_done", NT)
        var1_done = signal("var1_done", 1)
        rstd1_done = signal("rstd1_done", 1)
        xn1_done = signal("xn1_done", NT)
        x1t_done = signal("x1t_done", 1)
        x1_hi_done = signal("x1_hi_done", 1)
        x1_lo_done = signal("x1_lo_done", 1)
        x1_used = signal("x1_used", 1)
        rot_done = signal("rot_done", 4)
        qk_done = signal("qk_done", 2)
        qk_hi_done = signal("qk_hi_done", 2)
        qk_lo_done = signal("qk_lo_done", 2)
        v_hi_done = signal("v_hi_done", 1)
        v_lo_done = signal("v_lo_done", 1)
        tanh1_done = signal("tanh1_done", 1)
        router1 = signal("router1", 6)
        gate1_t_done = signal("gate1_t_done", 1)
        gate1_stored = signal("gate1_stored", 16)
        gates1_in = [signal(f"gates1_in_{r}", 16 * E // RING) for r in range(RING)]
        s1_full = signal("s1_full", 1)
        scores_done = signal("scores_done", 1)
        masked_done = signal("masked_done", NT)
        max_done = signal("max_done", NT)
        nmax_done = signal("nmax_done", 1)
        prob_done = signal("prob_done", NT)
        rsum_done = signal("rsum_done", 1)
        prob_normed = signal("prob_normed", NT)
        pt_hi_done = signal("pt_hi_done", 3)
        pt_lo_done = signal("pt_lo_done", 3)
        pv_done = signal("pv_done", 1)
        ctx_done = signal("ctx_done", 1)
        ctx_hi_done = signal("ctx_hi_done", 1)
        ctx_lo_done = signal("ctx_lo_done", 1)
        attn_done = signal("attn_done", 1)
        hs_relu_done = signal("hs_relu_done", 2)
        hs_done = signal("hs_done", 2)
        hs_hi_done = signal("hs_hi_done", 2)
        hs_lo_done = signal("hs_lo_done", 2)
        shared_down = signal("shared_down", 1)
        routed_in_done = signal("routed_in_done", E)
        relu16_done = signal("relu16_done", 12)
        hid16_done = signal("hid16_done", 12)
        pair_down = signal("pair_down", E // 2)
        g1_done = signal("g1_done", 1)
        sg1_done = signal("sg1_done", 1)
        y_done = signal("y_done", 1)
        y_stored = signal("y_stored", 16)

        for h in range(NH):
            G.read["up", h] = (silu_done, h + 1)
            U.read["up", h] = (mul_done, h + 1)
        G.read.update(b_tsg=(x1_done, 1), r_up=(tanh_done, 1), a_xt=(x0_hi_done, 1), a_gt=(gate0_t_done, 1))
        U.read.update(r_up=(tanh_done, 2), a_logits=(router0, 2))
        Z.read.update(b_xt=(x1_hi_done, 1), b_q=(rot_done, 1), b_qs=(rot_done, 2), b_k=(rot_done, 3),
                      b_ks=(rot_done, 4), b_route=(tanh1_done, 1), b_v=(v_lo_done, 1), b_su0=(hs_relu_done, 1),
                      b_su1=(hs_relu_done, 2), b_s02=(prob_done, 3), b_s3=(prob_done, 4), b_gt=(gate1_t_done, 1),
                      b_pt0=(pt_lo_done, 1), b_pt1=(pt_lo_done, 2), b_pt2=(pt_lo_done, 3), b_pv=(ctx_done, 1),
                      b_o=(attn_done, 1), b_out=(y_done, 1))
        for p in range(E // 2):
            for k, user in enumerate((f"b_u{2 * p}", f"b_u{2 * p + 1}", f"b_ur{p}")):
                Z.read[user] = (relu16_done, 3 * p + k + 1)

        def split_matmul(o, w, rhs_hi, rhs_lo, start, stop):
            nc.tensor.matmul(o, w[0], rhs_hi, start=start, stop=False)
            nc.tensor.matmul(o, w[0], rhs_lo, start=False, stop=False)
            return nc.tensor.matmul(o, w[1], rhs_hi, start=False, stop=stop)

        def weight(c, n=P):
            return w_hi[:, c:c + n], w_lo[:, c:c + n]

        def tok(n, m=1):
            return slice(n * P, (n + m) * P)

        def iterations(eng, run):
            run(At(0))
            run(At(1))
            with eng.Fori(1, NB // 2 - 1) as j:
                run(At(2 * j, 0))
                run(At(2 * j + 1, 1))
            run(At(NB - 2))
            run(At(NB - 1))
            run(At(NB))

        PROB = {t: slice(t * (t + 1) // 2 * P, (t + 1) * (t + 2) // 2 * P) for t in range(NT)}
        PT_AT = {0: (0, 0), 1: (1, 0), 3: (1, 3 * P), 2: (2, 0)}
        PT_OF = [[0], [1, 3], [2]]

        def score_bank(i, t):
            if t == 1:
                return y1[:, tok(0, 2)]
            if t == 3:
                return view(Z, i, "b_s3")[:, :]
            return view(Z, i, "b_s02")[:, tok(0) if t == 0 else tok(1, 3)]

        block = ctx.enter_context(nc.Block())

        @block.sync
        def _(sp):
            def load_x(b):
                rows = x[b.n:b.n + 1].rearrange("b (n p) d -> p (b n) d", p=P)
                sp.dma_start(x_in[:, b.parity], rows).then_inc(x_loaded[b.parity], 16)

            load_x(At(0))
            sp.dma_start(const[:], masks).then_inc(const_in, 16)
            for c in range(W_CHUNKS):
                if c >= 2:
                    sp.wait_ge(w_split, c - 1)
                sp.dma_start(w_stage[:, c % 2], weights[:, c * W_CHUNK:(c + 1) * W_CHUNK]).then_inc(w_in[c % 2], 16)
                if c == 0:
                    sp.dma_start(cols[:], columns).then_inc(cols_in, 16)
                    sp.dma_start(ties[:].rearrange("p a b -> p (a b)"), rank_ties).then_inc(ties_in, 16)
                    sp.dma_start(bias8[:], expert_bias.partition_broadcast(P)).then_inc(bias8_in, 16)
            sp.dma_start(cos_sin[:], rope).then_inc(rope_in, 16)
            for c in range(V_CHUNKS):
                if c >= 2:
                    sp.wait_ge(w16_cast, c - 1)
                sp.dma_start(gates1[:, c % 2 * 2:c % 2 * 2 + 2].rearrange("p r t -> p (r t)"),
                             weights16[:, c * V_CHUNK:(c + 1) * V_CHUNK]).then_inc(w16_in[c % 2], 16)

            def a_gt(i, b):
                sp.wait_ge(gate0_t_done, upto(gate0_t_done, b, 1))
                sp.dma_start(gate0_dram[b.parity].rearrange("(e t) -> e t", e=E), gate0_t[:]).then_inc(gate0_stored, 16)

            def spread0(e, at):
                def step(i, b):
                    sp.wait_ge(gated_done, upto(gated_done, b, 2 * (e - RING) + 2))
                    if e == 0:
                        sp.sem_inc(passed_sp, 1)
                        sp.wait_ge(gate0_stored, upto(gate0_stored, b, 16))
                    sp.dma_start(gates0[:, e % RING], gate0_dram[b.parity, e * T:(e + 1) * T].partition_broadcast(P)
                                 ).then_inc(gates0_in[e % RING], 16)
                return step

            def b_gt(i, b):
                sp.wait_ge(gate1_t_done, upto(gate1_t_done, b, 1))
                sp.dma_start(gate1_dram[b.parity].rearrange("(e t) -> e t", e=E), gate1_t[:]).then_inc(gate1_stored, 16)

            def spread1(e):
                def step(i, b):
                    sp.wait_ge(routed_in_done, upto(routed_in_done, b, e - RING + 1))
                    if e == 0:
                        sp.sem_inc(passed_sp, 1)
                        sp.wait_ge(gate1_stored, upto(gate1_stored, b, 16))
                    sp.dma_start(gates1[:, e % RING], gate1_dram[b.parity, e * T:(e + 1) * T].partition_broadcast(P)
                                 ).then_inc(gates1_in[e % RING], 16)
                return step

            def a_load(i, b):
                row = b.n if isinstance(b.n, int) else sp.snap(b.n)
                sp.wait_ge(x1_done, upto(x1_done, b + -1, 0))
                sp.dma_start(x_in[:, b.parity], x[bass.ds(row, 1)].rearrange("b (n p) d -> p (b n) d", p=P)
                             ).then_inc(x_loaded[b.parity], 16)

            def b_out(i, b):
                row = b.n if isinstance(b.n, int) else sp.snap(b.n)
                sp.wait_ge(y_done, upto(y_done, b, 1))
                sp.dma_start(out[bass.ds(row, 1)].rearrange("b (n p) d -> p (b n) d", p=P), y_out[:]
                             ).then_inc(y_stored, 16)

            STEPS = {"a_load": a_load, "a_gt": a_gt, "b_gt": b_gt, "b_out": b_out}
            for e in range(E):
                STEPS[f"a_g{e}" if e < RING else f"m_g{e}"] = spread0(e, 0)
                STEPS[f"b_g{e}"] = spread1(e)

            sp.wait_ge(w_split, W_CHUNKS)
            a_gt(At(-1), At(0))
            for e in range(RING):
                STEPS[f"a_g{e}"](At(-1), At(0))
            sp.wait_ge(w16_cast, V_CHUNKS)

            def run(i):
                for h in range(NH):
                    for part in range(3):
                        for s in steps(i, h, part):
                            if s in STEPS:
                                STEPS[s](i, i.batch(s))

            iterations(sp, run)
            sp.wait_ge(y_stored, 16 * NB)

        @block.tensor
        def _(pe):
            def a_xt(i, b):
                g = view(G, i, "a_xt")
                pe.wait_ge(*emptied(G, i, "a_xt"))
                pe.wait_ge(xn0_done, upto(xn0_done, b, NT))
                for n in range(NT):
                    last = nc.tensor.transpose(g[:, tok(n)], xn0[:, n, :], ident)
                last.then_inc(G.full, 1)

            def a_logits(i, b):
                u = view(U, i, "a_logits")
                pe.wait_ge(*emptied(U, i, "a_logits"))
                pe.wait_ge(x0_lo_done, upto(x0_lo_done, b, 1))
                w = weight(W_ROUTE0, E)
                for n in range(NT):
                    xh, xl = (x0[:, b.parity, tok(n)] for x0 in (x0_hi, x0_lo))
                    o = u[:, n * E:(n + 1) * E]
                    nc.tensor.matmul(o, xh, w[0], start=True, stop=False)
                    nc.tensor.matmul(o, xh, w[1], start=False, stop=False)
                    last = nc.tensor.matmul(o, xl, w[0], start=False, stop=True)
                last.then_inc(U.full, 1)

            def a_gt(i, b):
                g = view(G, i, "a_gt")
                pe.wait_ge(*emptied(G, i, "a_gt"))
                pe.wait_ge(router0, upto(router0, b, 13))
                for n in range(NT):
                    last = nc.tensor.transpose(g[0:E, tok(n)], gate0[:, n, :], ident)
                last.then_inc(G.full, 1)

            def r_up(i, b):
                g = view(G, i, "r_up")
                pe.wait_ge(*emptied(G, i, "r_up"))
                u = view(U, i, "r_up")
                pe.wait_ge(*emptied(U, i, "r_up"))
                xh, xl = x0_hi[:, b.parity], x0_lo[:, b.parity]
                split_matmul(g[:], weight(W_IG), xh, xl, True, True).then_inc(G.full, 1)
                split_matmul(u[:], weight(W_AG), xh, xl, True, True).then_inc(U.full, 1)

            def b_tsg(i, b):
                g = view(G, i, "b_tsg")
                pe.wait_ge(*emptied(G, i, "b_tsg"))
                pe.wait_ge(sg0_done, upto(sg0_done, b, 1))
                for n in range(NT):
                    last = nc.tensor.transpose(g[:, tok(n)], sg0[:, tok(n)], ident)
                last.then_inc(G.full, 1)

            def b_xt(i, b):
                z = view(Z, i, "b_xt")
                pe.wait_ge(*emptied(Z, i, "b_xt"))
                pe.wait_ge(xn1_done, upto(xn1_done, b, NT))
                for n in range(NT):
                    last = nc.tensor.transpose(z[:, tok(n)], xn1[:, n, :], ident)
                last.then_inc(Z.full, 1)

            def project(name, column):
                def step(i, b):
                    z = view(Z, i, name)
                    pe.wait_ge(*emptied(Z, i, name))
                    if name == "b_q":
                        pe.wait_ge(x1_lo_done, upto(x1_lo_done, b, 1))
                    split_matmul(z[:], weight(column), x1_hi[:], x1_lo[:], True, True).then_inc(Z.full, 1)
                return step

            def b_route(i, b):
                z = view(Z, i, "b_route")
                pe.wait_ge(*emptied(Z, i, "b_route"))
                w = weight(W_ROUTE1, E)
                for n in range(NT):
                    o = z[:, n * E:(n + 1) * E]
                    nc.tensor.matmul(o, x1_hi[:, tok(n)], w[0], start=True, stop=False)
                    nc.tensor.matmul(o, x1_hi[:, tok(n)], w[1], start=False, stop=False)
                    last = nc.tensor.matmul(o, x1_lo[:, tok(n)], w[0], start=False, stop=True)
                last.then_inc(Z.full, 1)

            def b_v(i, b):
                z = view(Z, i, "b_v")
                pe.wait_ge(*emptied(Z, i, "b_v"))
                w = weight(W_V)
                for n in range(NT):
                    o = z[:, tok(n)]
                    nc.tensor.matmul(o, x1_hi[:, tok(n)], w[0], start=True, stop=False)
                    nc.tensor.matmul(o, x1_hi[:, tok(n)], w[1], start=False, stop=False)
                    last = nc.tensor.matmul(o, x1_lo[:, tok(n)], w[0], start=False, stop=True)
                last.then_inc(Z.full, 1)

            def shared_up(j):
                def step(i, b):
                    z = view(Z, i, f"b_su{j}")
                    pe.wait_ge(*emptied(Z, i, f"b_su{j}"))
                    last = split_matmul(z[:], weight(W_SU + j * P), x1_hi[:], x1_lo[:], True, True)
                    last.then_inc(Z.full, 1)
                return step

            def scores_of(o, t):
                q = (q_hi[:, tok(t)], q_lo[:, tok(t)])
                return split_matmul(o, q, k_hi[:, tok(0, t + 1)], k_lo[:, tok(0, t + 1)], True, True)

            def b_s02(i, b):
                pe.wait_ge(*emptied(Z, i, "b_s02"))
                pe.wait_ge(qk_lo_done, upto(qk_lo_done, b, 2))
                scores_of(score_bank(i, 0), 0)
                scores_of(score_bank(i, 2), 2).then_inc(Z.full, 1)

            def b_s3(i, b):
                pe.wait_ge(*emptied(Z, i, "b_s3"))
                scores_of(score_bank(i, 3), 3).then_inc(Z.full, 1)

            def b_s1(i, b):
                pe.wait_ge(g1_done, upto(g1_done, b, 0))
                scores_of(score_bank(i, 1), 1).then_inc(s1_full, 1)

            def b_gt(i, b):
                z = view(Z, i, "b_gt")
                pe.wait_ge(*emptied(Z, i, "b_gt"))
                pe.wait_ge(router1, upto(router1, b, 6))
                for n in range(NT):
                    last = nc.tensor.transpose(z[0:E, tok(n)], gate1[:, n, :], ident)
                last.then_inc(Z.full, 1)

            def b_sd(i, b):
                pe.wait_ge(prob_done, upto(prob_done, b, NT))
                for j in range(2):
                    pe.wait_ge(hs_lo_done, upto(hs_lo_done, b, j + 1))
                    last = split_matmul(y1[:], weight(W_SD + j * P), hs_hi[j], hs_lo[j], j == 0, False)
                last.then_inc(shared_down, 1)

            def transposed_probs(m):
                def step(i, b):
                    z = view(Z, i, f"b_pt{m}")
                    pe.wait_ge(*emptied(Z, i, f"b_pt{m}"))
                    pe.wait_ge(prob_normed, upto(prob_normed, b, NT))
                    for s in PT_OF[m]:
                        at = PT_AT[s][1]
                        for t in range(s, NT):
                            src = prob[:, PROB[t].start + s * P:PROB[t].start + (s + 1) * P]
                            last = nc.tensor.transpose(z[:, at + (t - s) * P:at + (t - s + 1) * P], src, ident)
                    last.then_inc(Z.full, 1)
                return step

            def b_pv(i, b):
                z = view(Z, i, "b_pv")
                pe.wait_ge(*emptied(Z, i, "b_pv"))
                pe.wait_ge(v_lo_done, upto(v_lo_done, b, 1))
                pe.wait_ge(pt_lo_done, upto(pt_lo_done, b, 3))
                for s in range(NT):
                    m, at = PT_AT[s]
                    n = (NT - s) * P
                    v = (v_hi[:, tok(s)], v_lo[:, tok(s)])
                    last = split_matmul(z[:, s * P:T], v, pt_hi[:, m, at:at + n], pt_lo[:, m, at:at + n],
                                        s == 0, s == NT - 1)
                last.then_inc(Z.full, 1)

            def b_o(i, b):
                z = view(Z, i, "b_o")
                pe.wait_ge(*emptied(Z, i, "b_o"))
                pe.wait_ge(ctx_lo_done, upto(ctx_lo_done, b, 1))
                split_matmul(z[:], weight(W_O), ctx_hi[:], ctx_lo[:], True, True).then_inc(Z.full, 1)

            def routed_up(e):
                def step(i, b):
                    z = view(Z, i, f"b_u{e}")
                    pe.wait_ge(*emptied(Z, i, f"b_u{e}"))
                    pe.wait_ge(routed_in_done, upto(routed_in_done, b, e + 1))
                    nc.tensor.matmul(z[:], w16[:, V_U + e * P:V_U + (e + 1) * P], routed_in[:, e % 4],
                                     start=True, stop=True).then_inc(Z.full, 1)
                return step

            def routed_up_rest(p):
                def step(i, b):
                    z = view(Z, i, f"b_ur{p}")
                    pe.wait_ge(*emptied(Z, i, f"b_ur{p}"))
                    for k in range(2):
                        c = V_UR + p * P + k * HALF
                        last = nc.tensor.matmul(z[k * HALF:(k + 1) * HALF, :], w16[:, c:c + HALF],
                                                routed_in[:, (2 * p + k) % 4], start=True, stop=True)
                    last.then_inc(Z.full, 1)
                return step

            def routed_down(p):
                def step(i, b):
                    pe.wait_ge(hid16_done, upto(hid16_done, b, 3 * p + 3))
                    for k, c in enumerate((V_D + 2 * p * P, V_D + (2 * p + 1) * P, V_DR + p * P)):
                        last = nc.tensor.matmul(y1[:], w16[:, c:c + P], hid16[:, (3 * p + k) % 6],
                                                start=False, stop=(p == E // 2 - 1 and k == 2))
                    last.then_inc(pair_down, 1)
                return step

            def b_out(i, b):
                z = view(Z, i, "b_out")
                pe.wait_ge(*emptied(Z, i, "b_out"))
                pe.wait_ge(sg1_done, upto(sg1_done, b, 1))
                for n in range(NT):
                    last = nc.tensor.transpose(z[:, tok(n)], sg1[:, tok(n)], ident)
                last.then_inc(Z.full, 1)

            STEPS = {"a_xt": a_xt, "a_logits": a_logits, "a_gt": a_gt, "r_up": r_up, "b_tsg": b_tsg, "b_xt": b_xt,
                     "b_q": project("b_q", W_Q), "b_qs": project("b_qs", W_QS), "b_k": project("b_k", W_K),
                     "b_ks": project("b_ks", W_KS), "b_route": b_route, "b_v": b_v, "b_su0": shared_up(0),
                     "b_su1": shared_up(1), "b_s02": b_s02, "b_s3": b_s3, "b_s1": b_s1, "b_gt": b_gt, "b_sd": b_sd,
                     "b_pt0": transposed_probs(0), "b_pt1": transposed_probs(1), "b_pt2": transposed_probs(2),
                     "b_pv": b_pv, "b_o": b_o, "b_out": b_out}
            for e in range(E):
                STEPS[f"b_u{e}"] = routed_up(e)
            for p in range(E // 2):
                STEPS[f"b_ur{p}"] = routed_up_rest(p)
                STEPS[f"b_d{p}"] = routed_down(p)

            def up(i, h, which):
                ring = (G, U)[which]
                o = view(ring, i, ("up", h))
                pe.wait_ge(*emptied(ring, i, ("up", h)))
                c = W_GU + h // 2 * 2 * HID0 + which * HID0 + h % 2 * P
                split_matmul(o[:], weight(c), x0_hi[:, i.parity], x0_lo[:, i.parity], True, True).then_inc(ring.full, 1)

            def down(i, h):
                if h == 0:
                    pe.wait_ge(g0_done, upto(g0_done, i, 0))
                r = h % 3
                pe.wait_ge(lo_done[r], upto(lo_done[r], i, h // 3 + 1))
                split_matmul(y0[:], weight(W_D + h * P), hid_hi[:, r], hid_lo[:, r], h == 0,
                             h == NH - 1).then_inc(down_done, 1)

            def run(i):
                for h in range(NH):
                    for part in range(3):
                        if i.has("m"):
                            if part < 2:
                                up(i, h, part)
                            elif h >= LAG:
                                down(i, h - LAG)
                        for s in steps(i, h, part):
                            if s in STEPS:
                                STEPS[s](i, i.batch(s))
                if i.has("m"):
                    for h in range(NH - LAG, NH):
                        down(i, h)

            pe.wait_ge(const_in, 16)
            a_xt(At(-1), At(0))
            pe.wait_ge(w_split, 1)
            a_logits(At(-1), At(0))
            a_gt(At(-1), At(0))
            pe.wait_ge(w_split, W_CHUNKS)
            pe.wait_ge(w16_cast, V_CHUNKS)
            iterations(pe, run)

        @block.scalar
        def _(act):
            def a_xt(i, b):
                g = view(G, i, "a_xt")
                act.wait_ge(G.full, G.filled(i, "a_xt"))
                act.wait_ge(gated_x_done, upto(gated_x_done, b, 0))
                act.wait_ge(x0_lo_done, upto(x0_lo_done, b, 0))
                nc.scalar.copy(x0t[:], g[:]).then_inc(x0t_done, 1)
                act.wait_ge(down_done, upto(down_done, b + -1, 0))
                nc.scalar.copy(x0_hi[:, b.parity], g[:]).then_inc(x0_hi_done, 1)

            def a_exp(i, b):
                act.wait_ge(router0, upto(router0, b, 2))
                nc.scalar.activation(score0[:], logit[:], ACT.Exp).then_inc(exp0_done, 1)

            def a_gt(i, b):
                act.wait_ge(G.full, G.filled(i, "a_gt"))
                act.wait_ge(gate0_stored, upto(gate0_stored, b, 0))
                nc.scalar.copy(gate0_t[:], view(G, i, "a_gt")[0:E, :]).then_inc(gate0_t_done, 1)

            def r_up(i, b):
                act.wait_ge(G.full, G.filled(i, "r_up"))
                act.wait_ge(state_done, upto(state_done, b, 0))
                nc.scalar.activation(tanh_x[:], view(G, i, "r_up")[:], ACT.Tanh, bias=half_bias[:, 0:1],
                                     scale=0.5).then_inc(tanh_done, 1)
                act.wait_ge(U.full, U.filled(i, "r_up"))
                act.wait_ge(log_a_done, upto(log_a_done, b, 0))
                nc.scalar.activation(tanh_a[:], view(U, i, "r_up")[:], ACT.Tanh, bias=half_bias[:, 1:2],
                                     scale=0.5).then_inc(tanh_done, 1)

            def x_exp(i, b):
                if i.has("b"):
                    bb = i + -1
                    act.wait_ge(nmax_done, upto(nmax_done, bb, 1))
                    act.wait_ge(prob_normed, upto(prob_normed, bb, 0))
                    for t in range(NT):
                        if t == 0:
                            act.wait_ge(pt_lo_done, upto(pt_lo_done, bb, 0))
                        nc.scalar.activation(prob[:, PROB[t]], score_bank(i, t), ACT.Exp, bias=nmax[:, t:t + 1],
                                             scale=SCALE, accum_out=ssum[:, t:t + 1]).then_inc(prob_done, 1)
                if i.has("r"):
                    act.wait_ge(log_a_done, upto(log_a_done, i, 1))
                    act.wait_ge(normed_done, upto(normed_done, i, 0))
                    nc.scalar.activation(sq[:], log_a[:], ACT.Exp, scale=2.0).then_inc(a2_done, 1)
                    act.wait_ge(step_done, upto(step_done, i, 2))
                    nc.scalar.activation(step_a[:], step_a[:], ACT.Exp).then_inc(ratio_done, 1)
                if i.has("a"):
                    a_exp(i, i + 1)
                if i.has("r"):
                    act.wait_ge(room_done, upto(room_done, i, 1))
                    nc.scalar.activation(sq[:], sq[:], ACT.Sqrt, scale=-0.25).then_inc(root_done, 1)

            def b_silu(i, b):
                act.wait_ge(down_done, upto(down_done, b, NH))
                act.wait_ge(sg0_done, upto(sg0_done, b, 0))
                nc.scalar.activation(g0[:], y0[:], ACT.Silu).then_inc(g0_done, 1)

            def b_xt(i, b):
                z = view(Z, i, "b_xt")
                act.wait_ge(Z.full, Z.filled(i, "b_xt"))
                act.wait_ge(routed_in_done, upto(routed_in_done, b, 0))
                nc.scalar.copy(x1t[:], z[:]).then_inc(x1t_done, 1)
                nc.scalar.copy(x1_hi[:], z[:]).then_inc(x1_hi_done, 1)

            def b_qsum(i, b):
                act.wait_ge(qk_done, upto(qk_done, b, 1))
                nc.scalar.copy(q_hi, rot[:, 0]).then_inc(qk_hi_done, 1)

            def b_ksum(i, b):
                act.wait_ge(qk_done, upto(qk_done, b, 2))
                nc.scalar.copy(k_hi, rot[:, 2]).then_inc(qk_hi_done, 1)

            def b_v(i, b):
                act.wait_ge(Z.full, Z.filled(i, "b_v"))
                nc.scalar.copy(v_hi[:], view(Z, i, "b_v")[:]).then_inc(v_hi_done, 1)

            def b_route(i, b):
                act.wait_ge(Z.full, Z.filled(i, "b_route"))
                z = view(Z, i, "b_route")[:, 0:NT * E].rearrange("p (n e) -> p n e", e=E)
                nc.scalar.activation(tanh1[:], z, ACT.Tanh, scale=0.5).then_inc(tanh1_done, 1)

            def shared_up(j):
                def step(i, b):
                    act.wait_ge(Z.full, Z.filled(i, f"b_su{j}"))
                    nc.scalar.activation(hs[:, j], view(Z, i, f"b_su{j}")[:], ACT.Relu).then_inc(hs_relu_done, 1)
                return step

            def b_gt(i, b):
                for j in range(2):
                    act.wait_ge(hs_done, upto(hs_done, b, j + 1))
                    nc.scalar.copy(hs_hi[j], hs[:, j]).then_inc(hs_hi_done, 1)
                act.wait_ge(Z.full, Z.filled(i, "b_gt"))
                act.wait_ge(gate1_stored, upto(gate1_stored, b, 0))
                nc.scalar.copy(gate1_t[:], view(Z, i, "b_gt")[0:E, :]).then_inc(gate1_t_done, 1)

            def transposed_probs(m):
                n = sum(NT - s for s in PT_OF[m]) * P
                def step(i, b):
                    act.wait_ge(Z.full, Z.filled(i, f"b_pt{m}"))
                    nc.scalar.copy(pt_hi[:, m, 0:n], view(Z, i, f"b_pt{m}")[:, 0:n]).then_inc(pt_hi_done, 1)
                return step

            def b_pv(i, b):
                act.wait_ge(ctx_done, upto(ctx_done, b, 1))
                nc.scalar.copy(ctx_hi[:], ctxt[:]).then_inc(ctx_hi_done, 1)

            def b_o(i, b):
                act.wait_ge(Z.full, Z.filled(i, "b_o"))
                nc.scalar.activation(attn[:], view(Z, i, "b_o")[:], ACT.Identity,
                                     bias=cols[:, C_O:C_O + 1]).then_inc(attn_done, 1)

            def routed_up(name, k):
                def step(i, b):
                    act.wait_ge(Z.full, Z.filled(i, name))
                    act.wait_ge(hid16_done, upto(hid16_done, b, k - 1))
                    nc.scalar.activation(relu16[:, k % 2], view(Z, i, name)[:], ACT.Relu).then_inc(relu16_done, 1)
                return step

            def b_fin(i, b):
                act.wait_ge(pair_down, upto(pair_down, b, E // 2))
                nc.scalar.activation(g1, y1[:], ACT.Silu).then_inc(g1_done, 1)

            STEPS = {"a_xt": a_xt, "a_gt": a_gt, "r_up": r_up, "x_exp": x_exp, "b_silu": b_silu, "b_xt": b_xt,
                     "b_qsum": b_qsum, "b_ksum": b_ksum, "b_v": b_v, "b_route": b_route, "b_su0": shared_up(0),
                     "b_su1": shared_up(1), "b_gt": b_gt, "b_pt0": transposed_probs(0), "b_pt1": transposed_probs(1),
                     "b_pt2": transposed_probs(2), "b_pv": b_pv, "b_o": b_o, "b_fin": b_fin}
            for p in range(E // 2):
                for k, name in enumerate((f"b_u{2 * p}", f"b_u{2 * p + 1}", f"b_ur{p}")):
                    STEPS[name] = routed_up(name, 3 * p + k)

            def silu_of(i, h):
                act.wait_ge(G.full, G.filled(i, ("up", h)))
                act.wait_ge(mul_done, upto(mul_done, i, h - 1))
                nc.scalar.activation(silu[:, h % 2], view(G, i, ("up", h))[:], ACT.Silu).then_inc(silu_done, 1)

            def round_hid(i, h):
                if h < 2:
                    act.wait_ge(mul_done, upto(mul_done, i, h + 1))
                else:
                    act.wait_ge(gated_done, upto(gated_done, i, h - 1))
                act.wait_ge(down_done, upto(down_done, i, h - 2))
                nc.scalar.copy(hid_hi[:, h % 3], hid[:, h % 3]).then_inc(hi_done, 1)

            def run(i):
                for h in range(NH):
                    if i.has("m"):
                        silu_of(i, h)
                    for part in range(3):
                        if i.has("m") and part == 1 and h >= 1:
                            round_hid(i, h - 1)
                        for s in steps(i, h, part):
                            if s in STEPS:
                                STEPS[s](i, i.batch(s))
                if i.has("m"):
                    round_hid(i, NH - 1)

            for c in range(W_CHUNKS):
                if c == 1:
                    a_xt(At(-1), At(0))
                act.wait_ge(w_in[c % 2], 16 * (c // 2 + 1))
                nc.scalar.copy(w_hi[:, c * W_CHUNK:(c + 1) * W_CHUNK], w_stage[:, c % 2]).then_inc(w_rounded, 1)
            a_exp(At(-1), At(0))
            act.wait_ge(soft_dve, 1)
            nc.scalar.activation(decay[:, 1:2], decay[:, 0:1], ACT.Exp, scale=-1.0).then_inc(soft_act, 1)
            act.wait_ge(soft_act, 1)
            nc.scalar.activation(decay[:, 2:3], decay[:, 1:2], ACT.Ln, bias=1.0).then_inc(soft_act, 1)
            a_gt(At(-1), At(0))
            act.wait_ge(half_set, 2)
            iterations(act, run)

        @block.vector
        def _(dve):
            def layernorm(b, src, stats, mv, var, rstd, dst, stats_done, mv_done, var_done, rstd_done, dst_done):
                for n in range(NT):
                    nc.vector.bn_stats(stats[:, n, :], src[:, n, :]).then_inc(stats_done, 1)
                dve.wait_ge(dst_done, upto(dst_done, b, 0))
                dve.wait_ge(stats_done, upto(stats_done, b, NT))
                dve.sem_inc(passed_dve, 1)
                for n in range(NT):
                    nc.vector.bn_aggr(mv[:, n, :], stats[:, n, :]).then_inc(mv_done, 1)
                dve.wait_ge(mv_done, upto(mv_done, b, NT))
                dve.wait_ge(rstd_done, upto(rstd_done, b, 0))
                nc.vector.tensor_scalar_add(var[:], mv[:, :, 1], EPS).then_inc(var_done, 1)
                dve.wait_ge(rstd_done, upto(rstd_done, b, 1))
                for n in range(NT):
                    nc.vector.tensor_scalar(dst[:, n, :], src[:, n, :], mv[:, n, 0:1], rstd[:, n:n + 1],
                                            ALU.subtract, ALU.mult).then_inc(dst_done, 1)

            def wide(a, axis):
                return a.unsqueeze(axis).to_broadcast([P, NT, E, E])

            def ranks(b, s, values, beats, rank, k):
                nc.vector.tensor_tensor(beats[:], wide(values, 2), wide(values, 3), ALU.subtract).then_inc(s, 1)
                dve.wait_ge(s, upto(s, b, k + 1))
                nc.vector.tensor_tensor(beats[:], beats[:], ties[:].unsqueeze(1).to_broadcast([P, NT, E, E]),
                                        ALU.is_gt).then_inc(s, 1)
                dve.wait_ge(s, upto(s, b, k + 2))
                nc.vector.reduce_sum(rank[:], beats[:], axis=AX.X).then_inc(s, 1)
                dve.wait_ge(s, upto(s, b, k + 3))

            def a_norm(i, b):
                half = b.parity
                dve.wait_ge(x_loaded[half], upto(x_loaded[half], b, 16 - 8 * half))
                dve.wait_ge(x0t_done, upto(x0t_done, b, 0))
                layernorm(b, x_in[:, half], stats0, mv0, var0, rstd0, xn0,
                          stats0_done, mv0_done, var0_done, rstd0_done, xn0_done)

            def a_logits(i, b):
                z = view(U, i, "a_logits")[:, 0:NT * E].rearrange("p (n e) -> p n e", e=E)
                dve.wait_ge(U.full, U.filled(i, "a_logits"))
                nc.vector.reduce_max(top[:, :, 0], z, axis=AX.X).then_inc(router0, 1)
                dve.wait_ge(router0, upto(router0, b, 1))
                nc.vector.tensor_tensor(logit[:], z, top[:, :, 0:1].to_broadcast([P, NT, E]),
                                        ALU.subtract).then_inc(router0, 1)

            def a_gate(i, b):
                dve.wait_ge(exp0_done, upto(exp0_done, b, 1))
                nc.vector.reduce_sum(top[:, :, 1], score0[:], axis=AX.X).then_inc(router0, 1)
                dve.wait_ge(router0, upto(router0, b, 3))
                nc.vector.reciprocal(top[:, :, 2], top[:, :, 1]).then_inc(router0, 1)
                dve.wait_ge(router0, upto(router0, b, 4))
                nc.vector.tensor_tensor(score0[:], score0[:], top[:, :, 2:3].to_broadcast([P, NT, E]),
                                        ALU.mult).then_inc(router0, 1)
                dve.wait_ge(router0, upto(router0, b, 5))
                ranks(b, router0, score0[:], beats, rank, 5)
                nc.vector.scalar_tensor_tensor(score0[:], rank[:], 2.0, score0[:], ALU.is_lt,
                                               ALU.mult).then_inc(router0, 1)
                dve.wait_ge(router0, upto(router0, b, 9))
                nc.vector.reduce_sum(top[:, :, 1], score0[:], axis=AX.X).then_inc(router0, 1)
                dve.wait_ge(router0, upto(router0, b, 10))
                nc.vector.tensor_scalar_add(top[:, :, 3], top[:, :, 1], 1e-20).then_inc(router0, 1)
                dve.wait_ge(router0, upto(router0, b, 11))
                nc.vector.reciprocal(top[:, :, 2], top[:, :, 3]).then_inc(router0, 1)
                dve.wait_ge(router0, upto(router0, b, 12))
                dve.wait_ge(gate0_t_done, upto(gate0_t_done, b, 0))
                nc.vector.tensor_tensor(gate0[:], score0[:], top[:, :, 2:3].to_broadcast([P, NT, E]),
                                        ALU.mult).then_inc(router0, 1)

            def r_scan(i, b):
                dve.wait_ge(tanh_done, upto(tanh_done, b, 2))
                dve.wait_ge(a2_done, upto(a2_done, b, 0))
                nc.vector.tensor_scalar(log_a[:], tanh_a[:], 1.0, decay[:, 5:6], ALU.add, ALU.mult).then_inc(log_a_done, 1)
                dve.wait_ge(log_a_done, upto(log_a_done, b, 1))
                dve.wait_ge(normed_done, upto(normed_done, b, 0))
                nc.vector.memset(level[:, 0:1], 0.0).then_inc(level_done, 1)
                nc.vector.tensor_tensor_scan(level[:, 1:T], log_a[:, 0:T - 1],
                                             ln_floor[:].to_broadcast([P, T - 1]), 0.0,
                                             ALU.add, ALU.max).then_inc(level_done, 1)
                dve.wait_ge(level_done, upto(level_done, b, 2))
                dve.wait_ge(state_done, upto(state_done, b, 0))
                nc.vector.tensor_tensor(step_a[:, 1:T], level[:, 1:T], level[:, 0:T - 1],
                                        ALU.subtract).then_inc(step_done, 1)
                nc.vector.memset(step_a[:, 0:1], 0.0).then_inc(step_done, 1)
                dve.wait_ge(x0t_done, upto(x0t_done, b, 1))
                nc.vector.scalar_tensor_tensor(normed[:], tanh_x[:], 1.0, x0t[:], ALU.add, ALU.mult).then_inc(gated_x_done, 1)

            def x_exp(i, b):
                if i.has("r"):
                    dve.wait_ge(a2_done, upto(a2_done, i, 1))
                    nc.vector.tensor_scalar(sq[:], sq[:], -1.0, -FLOOR, ALU.add, ALU.min).then_inc(room_done, 1)

            def r_fin(i, b):
                dve.wait_ge(root_done, upto(root_done, b, 1))
                nc.vector.tensor_tensor(normed[:], normed[:], sq[:], ALU.mult).then_inc(normed_done, 1)
                dve.wait_ge(normed_done, upto(normed_done, b, 1))
                dve.wait_ge(ratio_done, upto(ratio_done, b, 1))
                dve.wait_ge(sg0_done, upto(sg0_done, b, 0))
                nc.vector.tensor_tensor_scan(state[:], step_a[:], normed[:], 0.0, ALU.mult, ALU.add).then_inc(state_done, 1)

            def b_silu(i, b):
                dve.wait_ge(g0_done, upto(g0_done, b, 1))
                dve.wait_ge(state_done, upto(state_done, b, 1))
                dve.wait_ge(x1_done, upto(x1_done, b, 0))
                nc.vector.tensor_tensor(sg0[:], state[:], g0[:], ALU.mult).then_inc(sg0_done, 1)

            def b_tsg(i, b):
                dve.wait_ge(y_stored, upto(y_stored, b, 0))
                dve.wait_ge(G.full, G.filled(i, "b_tsg"))
                g = view(G, i, "b_tsg")[:].rearrange("p (n d) -> p n d", d=P)
                nc.vector.tensor_tensor(x1[:], x_in[:, b.parity], g, ALU.add).then_inc(x1_done, 1)
                dve.wait_ge(x1_done, upto(x1_done, b, 1))
                dve.wait_ge(x1t_done, upto(x1t_done, b, 0))
                layernorm(b, x1, stats1, mv1, var1, rstd1, xn1,
                          stats1_done, mv1_done, var1_done, rstd1_done, xn1_done)

            def rotated(name, k, column):
                def step(i, b):
                    dve.wait_ge(Z.full, Z.filled(i, name))
                    if k % 2 == 0:
                        dve.wait_ge(qk_lo_done, upto(qk_lo_done, b, 0))
                    nc.vector.scalar_tensor_tensor(rot[:, k], view(Z, i, name)[:], cols[:, column:column + 1],
                                                   cos_sin[:, k % 2], ALU.add, ALU.mult).then_inc(rot_done, 1)
                return step

            def b_v(i, b):
                dve.wait_ge(v_hi_done, upto(v_hi_done, b, 1))
                nc.vector.tensor_tensor(v_lo[:], view(Z, i, "b_v")[:], v_hi[:].bitcast(F32), ALU.subtract).then_inc(v_lo_done, 1)

            def b_ksum(i, b):
                dve.wait_ge(tanh1_done, upto(tanh1_done, b, 1))
                nc.vector.tensor_scalar(score1[:], tanh1[:], 0.5, 0.5, ALU.mult, ALU.add).then_inc(router1, 1)
                dve.wait_ge(router1, upto(router1, b, 1))
                nc.vector.tensor_tensor(biased[:], score1[:], bias8[:].unsqueeze(1).to_broadcast([P, NT, E]),
                                        ALU.add).then_inc(router1, 1)
                dve.wait_ge(router1, upto(router1, b, 2))
                ranks(b, router1, biased[:], beats1, rank1, 2)
                dve.wait_ge(gate1_t_done, upto(gate1_t_done, b, 0))
                nc.vector.scalar_tensor_tensor(gate1[:], rank1[:], 2.0, score1[:], ALU.is_lt,
                                               ALU.mult).then_inc(router1, 1)

            def mask_and_max(i, b, t, k):
                o = score_bank(i, t)
                nc.vector.tensor_tensor(o[:, tok(t)], o[:, tok(t)], causal, ALU.add).then_inc(masked_done, 1)
                dve.wait_ge(masked_done, upto(masked_done, b, k + 1))
                nc.vector.reduce_max(smax[:, t:t + 1], o, axis=AX.X).then_inc(max_done, 1)

            def b_s02(i, b):
                dve.wait_ge(Z.full, Z.filled(i, "b_s02"))
                mask_and_max(i, b, 0, 0)
                mask_and_max(i, b, 2, 1)

            def b_s3(i, b):
                dve.wait_ge(Z.full, Z.filled(i, "b_s3"))
                mask_and_max(i, b, 3, 2)

            def b_s1(i, b):
                dve.wait_ge(s1_full, upto(s1_full, b, 1))
                mask_and_max(i, b, 1, 3)
                dve.wait_ge(max_done, upto(max_done, b, NT))
                nc.vector.tensor_scalar_mul(nmax, smax, -SCALE).then_inc(nmax_done, 1)

            def b_pn(i, b):
                dve.wait_ge(prob_done, upto(prob_done, b, NT))
                nc.vector.reciprocal(rsum, ssum).then_inc(rsum_done, 1)
                dve.wait_ge(rsum_done, upto(rsum_done, b, 1))
                for t in range(NT):
                    nc.vector.tensor_scalar_mul(prob[:, PROB[t]], prob[:, PROB[t]], rsum[:, t:t + 1]).then_inc(prob_normed, 1)

            def transposed_probs(m):
                n = sum(NT - s for s in PT_OF[m]) * P
                def step(i, b):
                    dve.wait_ge(pt_hi_done, upto(pt_hi_done, b, m + 1))
                    nc.vector.tensor_tensor(pt_lo[:, m, 0:n], view(Z, i, f"b_pt{m}")[:, 0:n],
                                            pt_hi[:, m, 0:n].bitcast(F32), ALU.subtract).then_inc(pt_lo_done, 1)
                return step

            def b_pv(i, b):
                dve.wait_ge(Z.full, Z.filled(i, "b_pv"))
                dve.wait_ge(ctx_lo_done, upto(ctx_lo_done, b, 0))
                nc.vector.tensor_scalar_add(ctxt[:], view(Z, i, "b_pv")[:], cols[:, C_V:C_V + 1]).then_inc(ctx_done, 1)

            def gated_inputs(p):
                def step(i, b):
                    if p == 0:
                        dve.wait_ge(x1t_done, upto(x1t_done, b, 1))
                    for e in (2 * p, 2 * p + 1):
                        dve.wait_ge(relu16_done, upto(relu16_done, b, 3 * (p - 1)))
                        dve.wait_ge(gates1_in[e % RING], upto(gates1_in[e % RING], b, 16 * (e // RING + 1)))
                        nc.vector.tensor_tensor(routed_in[:, e % 4], x1t[:], gates1[:, e % RING], ALU.mult).then_inc(routed_in_done, 1)
                return step

            def routed_up(name, k):
                def step(i, b):
                    dve.wait_ge(relu16_done, upto(relu16_done, b, k + 1))
                    dve.wait_ge(pair_down, upto(pair_down, b, k // 3 - 1))
                    nc.vector.tensor_tensor(hid16[:, k % 6], relu16[:, k % 2], relu16[:, k % 2], ALU.mult).then_inc(hid16_done, 1)
                return step

            def b_fin(i, b):
                dve.wait_ge(g1_done, upto(g1_done, b, 1))
                dve.wait_ge(attn_done, upto(attn_done, b, 1))
                nc.vector.tensor_tensor(sg1, attn[:], g1, ALU.mult).then_inc(sg1_done, 1)

            def b_out(i, b):
                dve.wait_ge(Z.full, Z.filled(i, "b_out"))
                z = view(Z, i, "b_out")[:].rearrange("p (n d) -> p n d", d=P)
                nc.vector.tensor_tensor(y_out[:], x1[:], z, ALU.add).then_inc(y_done, 1)

            STEPS = {"a_norm": a_norm, "a_logits": a_logits, "a_gate": a_gate, "r_scan": r_scan, "x_exp": x_exp,
                     "r_fin": r_fin, "b_silu": b_silu, "b_tsg": b_tsg, "b_q": rotated("b_q", 0, C_Q),
                     "b_qs": rotated("b_qs", 1, C_QS), "b_k": rotated("b_k", 2, C_K), "b_ks": rotated("b_ks", 3, C_KS),
                     "b_v": b_v, "b_ksum": b_ksum, "b_s02": b_s02, "b_s3": b_s3, "b_s1": b_s1, "b_pn": b_pn,
                     "b_pt0": transposed_probs(0), "b_pt1": transposed_probs(1), "b_pt2": transposed_probs(2),
                     "b_pv": b_pv, "b_fin": b_fin, "b_out": b_out}
            for p in range(E // 2):
                STEPS[f"b_x{p}"] = gated_inputs(p)
                for k, name in enumerate((f"b_u{2 * p}", f"b_u{2 * p + 1}", f"b_ur{p}")):
                    STEPS[name] = routed_up(name, 3 * p + k)

            def multiply(i, h):
                dve.wait_ge(silu_done, upto(silu_done, i, h + 1))
                dve.wait_ge(U.full, U.filled(i, ("up", h)))
                dve.wait_ge(lo_done[h % 3], upto(lo_done[h % 3], i, h // 3))
                nc.vector.tensor_tensor(hid[:, h % 3], silu[:, h % 2], view(U, i, ("up", h))[:], ALU.mult).then_inc(mul_done, 1)

            def rest_of_hid(i, h):
                dve.wait_ge(hi_done, upto(hi_done, i, h + 1))
                dve.wait_ge(down_done, upto(down_done, i, h - 2))
                nc.vector.tensor_tensor(hid_lo[:, 2], hid[:, 2], hid_hi[:, 2].bitcast(F32), ALU.subtract).then_inc(lo_done[2], 1)

            def run(i):
                for h in range(NH):
                    if i.has("m"):
                        multiply(i, h)
                    for part in range(3):
                        if i.has("m") and part == 1 and h >= 1 and (h - 1) % 3 == 2:
                            rest_of_hid(i, h - 1)
                        for s in steps(i, h, part):
                            if s in STEPS:
                                STEPS[s](i, i.batch(s))
                if i.has("m"):
                    rest_of_hid(i, NH - 1)

            nc.vector.memset(ln_floor[:], LN_FLOOR).then_inc(const_set, 1)
            nc.vector.memset(minus_half[:], -0.5).then_inc(const_set, 1)
            a_norm(At(-1), At(0))
            for c in range(W_CHUNKS):
                dve.wait_ge(w_rounded, c + 1)
                part = slice(c * W_CHUNK, (c + 1) * W_CHUNK)
                nc.vector.tensor_tensor(w_lo[:, part], w_stage[:, c % 2], w_hi[:, part].bitcast(F32),
                                        ALU.subtract).then_inc(w_split, 1)
                if c == 1:
                    dve.wait_ge(cols_in, 16)
                    nc.vector.scalar_tensor_tensor(decay[:, 0:1], cols[:, C_A:C_A + 1], -1.0, cols[:, C_A:C_A + 1],
                                                   ALU.mult, ALU.max).then_inc(soft_dve, 1)
                    nc.vector.tensor_scalar_mul(half_bias[:], cols[:, C_IG:C_AG + 1], 0.5).then_inc(half_set, 1)
                    a_logits(At(-1), At(0))
            dve.wait_ge(ties_in, 16)
            dve.wait_ge(bias8_in, 16)
            a_gate(At(-1), At(0))
            dve.wait_ge(soft_act, 2)
            nc.vector.tensor_scalar_max(decay[:, 3:4], cols[:, C_A:C_A + 1], 0.0).then_inc(soft_dve, 1)
            dve.wait_ge(soft_dve, 2)
            nc.vector.tensor_tensor(decay[:, 4:5], decay[:, 3:4], decay[:, 2:3], ALU.add).then_inc(soft_dve, 1)
            dve.wait_ge(soft_dve, 3)
            nc.vector.tensor_scalar_mul(decay[:, 5:6], decay[:, 4:5], -4.0).then_inc(half_set, 1)
            dve.wait_ge(half_set, 2)
            dve.wait_ge(const_set, 2)
            dve.wait_ge(rope_in, 16)
            dve.wait_ge(const_in, 16)
            iterations(dve, run)

        @block.gpsimd
        def _(pool):
            TT = nc.gpsimd.tensor_tensor

            def a_norm(i, b):
                pool.wait_ge(var0_done, upto(var0_done, b, 1))
                pool.wait_ge(xn0_done, upto(xn0_done, b, 0))
                TT(rstd0[:], var0[:], minus_half[:], ALU.pow).then_inc(rstd0_done, 1)

            def a_xt(i, b):
                pool.wait_ge(x0t_done, upto(x0t_done, b, 1))
                pool.wait_ge(x0_hi_done, upto(x0_hi_done, b, 1))
                TT(x0_lo[:, b.parity], x0t[:], x0_hi[:, b.parity].bitcast(F32), ALU.subtract).then_inc(x0_lo_done, 1)

            def b_tsg(i, b):
                pool.wait_ge(var1_done, upto(var1_done, b, 1))
                pool.wait_ge(xn1_done, upto(xn1_done, b, 0))
                TT(rstd1[:], var1[:], minus_half[:], ALU.pow).then_inc(rstd1_done, 1)

            def b_xt(i, b):
                pool.wait_ge(x1t_done, upto(x1t_done, b, 1))
                pool.wait_ge(x1_hi_done, upto(x1_hi_done, b, 1))
                TT(x1_lo[:], x1t[:], x1_hi[:].bitcast(F32), ALU.subtract).then_inc(x1_lo_done, 1)

            def rotated_sum(k, hi, lo):
                def step(i, b):
                    pool.wait_ge(rot_done, upto(rot_done, b, 2 * k + 2))
                    TT(rot[:, 2 * k], rot[:, 2 * k], rot[:, 2 * k + 1], ALU.add).then_inc(qk_done, 1)
                    pool.wait_ge(qk_hi_done, upto(qk_hi_done, b, k + 1))
                    TT(lo, rot[:, 2 * k], hi.bitcast(F32), ALU.subtract).then_inc(qk_lo_done, 1)
                return step

            def shared_up(j):
                def step(i, b):
                    pool.wait_ge(hs_relu_done, upto(hs_relu_done, b, j + 1))
                    TT(hs[:, j], hs[:, j], hs[:, j], ALU.mult).then_inc(hs_done, 1)
                return step

            def b_gt(i, b):
                for j in range(2):
                    pool.wait_ge(hs_hi_done, upto(hs_hi_done, b, j + 1))
                    TT(hs_lo[j], hs[:, j], hs_hi[j].bitcast(F32), ALU.subtract).then_inc(hs_lo_done, 1)

            def b_pv(i, b):
                pool.wait_ge(ctx_hi_done, upto(ctx_hi_done, b, 1))
                TT(ctx_lo[:], ctxt[:], ctx_hi[:].bitcast(F32), ALU.subtract).then_inc(ctx_lo_done, 1)

            STEPS = {"a_norm": a_norm, "a_xt": a_xt, "b_tsg": b_tsg, "b_xt": b_xt,
                     "b_qsum": rotated_sum(0, q_hi, q_lo), "b_ksum": rotated_sum(1, k_hi, k_lo),
                     "b_su0": shared_up(0), "b_su1": shared_up(1), "b_gt": b_gt, "b_pv": b_pv}

            def gate(i, h):
                e = h // 2 - 1
                pool.wait_ge(gates0_in[e % RING], upto(gates0_in[e % RING], i, 16 * (e // RING + 1)))
                pool.wait_ge(mul_done, upto(mul_done, i, h + 1))
                r = h % 3
                TT(hid[:, r], hid[:, r], gates0[:, e % RING], ALU.mult).then_inc(gated_done, 1)

            def rest_of_hid(i, h):
                pool.wait_ge(hi_done, upto(hi_done, i, h + 1))
                pool.wait_ge(down_done, upto(down_done, i, h - 2))
                r = h % 3
                TT(hid_lo[:, r], hid[:, r], hid_hi[:, r].bitcast(F32), ALU.subtract).then_inc(lo_done[r], 1)

            def run(i):
                for h in range(NH):
                    if i.has("m") and h >= 2:
                        gate(i, h)
                    for part in range(3):
                        if i.has("m") and part == 1 and h >= 1 and (h - 1) % 3 < 2:
                            rest_of_hid(i, h - 1)
                        for s in steps(i, h, part):
                            if s in STEPS:
                                STEPS[s](i, i.batch(s))

            pool.wait_ge(const_set, 2)
            a_norm(At(-1), At(0))
            a_xt(At(-1), At(0))
            for c in range(V_CHUNKS):
                pool.wait_ge(w16_in[c % 2], 16 * (c // 2 + 1))
                nc.gpsimd.tensor_copy(w16[:, c * V_CHUNK:(c + 1) * V_CHUNK],
                                      gates1[:, c % 2 * 2:c % 2 * 2 + 2].rearrange("p r t -> p (r t)")
                                      ).then_inc(w16_cast, 1)
            iterations(pool, run)


def kernel(**inputs):
    import numpy as np
    import concourse.bacc as _bacc
    from concourse import mybir as _mybir
    from concourse.bass_utils import run_bass_kernel_spmd as _run

    a = {k: np.asarray(v) for k, v in inputs.items()}
    f32 = np.float32

    def block_diagonal(w):
        out = np.zeros((P, P), f32)
        n = w.shape[1]
        for h in range(w.shape[0]):
            out[h * n:(h + 1) * n, h * n:(h + 1) * n] = w[h]
        return out

    def swapped(w):
        return w.reshape(*w.shape[:-1], -1, 2)[..., ::-1].reshape(w.shape)

    up0 = [np.concatenate([a["L0_ffn_Sg"], a["L0_ffn_Su"]], 1)]
    up0 += [np.concatenate([a["L0_ffn_Wg"][e], a["L0_ffn_Wu"][e]], 1) for e in range(E)]
    down0 = [w.reshape(HID0 // P, P, P).transpose(1, 0, 2).reshape(P, HID0)
             for w in [a["L0_ffn_Sd"], *a["L0_ffn_Wd"]]]
    shared_up = np.zeros((P, 2 * P), f32)
    shared_up[:, :HID1] = a["L1_ffn_shared_w_up"].T
    shared_down = np.zeros((2 * P, P), f32)
    shared_down[:HID1] = a["L1_ffn_shared_w_down"].T
    shared_down = shared_down.reshape(2, P, P).transpose(1, 0, 2).reshape(P, 2 * P)
    weights = np.concatenate(
        [a["L0_ffn_Wr"], a["L1_ffn_gate_w"].T, block_diagonal(a["L0_attn_ig_w"]), block_diagonal(a["L0_attn_ag_w"]),
         *up0, *down0, a["L1_attn_Wq"], swapped(a["L1_attn_Wq"]), a["L1_attn_Wk"], swapped(a["L1_attn_Wk"]),
         a["L1_attn_Wv"], a["L1_attn_Wo"], shared_up, shared_down], 1)

    w_up, w_down = a["L1_ffn_w_up"], a["L1_ffn_w_down"]
    rest_up = np.zeros((P, E, HALF), f32)
    rest_down = np.zeros((E, HALF, P), f32)
    for e in range(E):
        rest_up[:, e, :REM] = w_up[e, P:, :].T
        rest_down[e, :REM] = w_down[e, :, P:].T
    weights16 = np.concatenate(
        [w_up[:, :P, :].transpose(2, 0, 1).reshape(P, E * P), rest_up.reshape(P, E * HALF),
         w_down[:, :, :P].transpose(2, 0, 1).reshape(P, E * P),
         rest_down.reshape(E // 2, P, P).transpose(1, 0, 2).reshape(P, E // 2 * P)], 1)

    columns = np.stack(
        [a["L0_attn_ig_b"].reshape(P), a["L0_attn_ag_b"].reshape(P), a["L0_attn_a_param"], a["L1_attn_bq"],
         swapped(a["L1_attn_bq"]), a["L1_attn_bk"], swapped(a["L1_attn_bk"]), a["L1_attn_bv"], a["L1_attn_bo"]], 1)

    inv_freq = (f32(1.0) / f32(10000.0) ** (np.arange(0, P, 2, dtype=f32) / f32(P))).astype(f32)
    angles = np.repeat(np.arange(T, dtype=f32)[None, :] * inv_freq[:, None], 2, axis=0)
    sign = np.where(np.arange(P) % 2 == 0, -1.0, 1.0).astype(f32)[:, None]
    rope = np.stack([np.cos(angles), np.sin(angles) * sign], 1).astype(f32)
    masks = np.stack([np.eye(P, dtype=f32), np.triu(np.full((P, P), MASKED, f32), 1)], 1)
    n = np.arange(E)
    rank_ties = np.tile(np.where(n[None, :] < n[:, None], -1e-37, 0.0).astype(f32).reshape(1, E * E), (P, 1))

    nc = _bacc.Bacc("TRN2", target_bir_lowering=False, num_devices=1)
    arrays, args = {}, []
    for name, v in [("x", a["L0_attn_x"]), ("weights", weights), ("weights16", weights16), ("columns", columns),
                    ("rope", rope), ("masks", masks), ("rank_ties", rank_ties),
                    ("expert_bias", a["L1_ffn_expert_bias"])]:
        v = np.ascontiguousarray(v)
        arrays[name] = v
        args.append(nc.dram_tensor(name, v.shape, _mybir.dt.from_np(v.dtype), kind="ExternalInput").ap())
    args.append(nc.dram_tensor("out", (NB, T, P), _mybir.dt.float32, kind="ExternalOutput").ap())
    build_layers(nc, *args)
    return _run(nc, [arrays], core_ids=[0]).results[0]["out"]
```

```python
import concourse.bass as bass
from concourse import mybir
from contextlib import ExitStack

P = 128
NB = 16
T = 512
NT = T // P
E = 8
HID0 = 256
HID1 = 176
REM = HID1 - P
HALF = 64
NH = (E + 1) * HID0 // P
EPS = 1e-5
FLOOR = 1e-7
LN_FLOOR = -16.11809565095832
MASKED = -1e37

W_ROUTE0 = 0
W_ROUTE1 = W_ROUTE0 + E
W_IG = W_ROUTE1 + E
W_AG = W_IG + P
W_EXPERT = W_AG + P
EXPERT = 3 * HID0
W_Q = W_EXPERT + (E + 1) * EXPERT
W_QS, W_K, W_KS, W_V, W_O = (W_Q + P * n for n in range(1, 6))
W_SU = W_O + P
W_SD = W_SU + 2 * P
W_ALL = W_SD + 2 * P
W_BOUNDS = [0, *(W_EXPERT + EXPERT * e for e in range(E + 2)), (W_Q + W_ALL) // 2, W_ALL]
W_CHUNKS = len(W_BOUNDS) - 1
V_U = 0
V_UR = V_U + E * P
V_D = V_UR + E // 2 * P
V_DR = V_D + E * P
V_ALL = V_DR + E // 2 * P
V_CHUNK = EXPERT
V_CHUNKS = V_ALL // V_CHUNK
C_IG, C_AG, C_A, C_Q, C_QS, C_K, C_KS, C_V, C_O, C_N = range(10)

SCHEDULE = {
    "pe": """3 c_u4 6 c_u5 7 c_ur2 11 b_tsg 11 r_up 13 c_d2 14 c_u6 15 c_u7 16 b_xt 16 c_ur3 20 c_d3 22 b_q 22 b_qs
        24 b_k 24 a_xt 24 b_ks 25 b_v 26 b_route 26 c_out 28 b_su0 29 b_su1 29 a_logits 31 b_s02 32 b_s3 32 b_s1
        34 b_gt 37 b_pt0 40 b_sd 40 b_pt1 40 a_gt 40 b_pt2 41 b_u0 43 b_u1 43 b_pv 45 b_ur0 46 b_o 48 b_d0
        48 b_u2 49 b_u3 51 b_ur1 53 b_d1""",
    "act": """2 c_u4 6 c_u5 7 c_ur2 8 b_silu 13 r_up 13 c_u6 14 c_u7 16 c_ur3 18 b_xt 20 c_fin 25 a_xt 25 b_qsum 25 b_v
        26 b_route 27 b_ksum 28 b_su0 31 b_su1 31 b_sq0 31 b_hhi0 31 b_sq1 33 a_exp 33 b_prob 33 r_exp 34 b_hhi1
        34 b_gt 35 r_root 37 b_pt0 39 b_pt1 39 b_pt2 40 b_u0 42 a_gt 43 b_u1 44 b_pv 45 b_ur0 45 b_o 46 b_u2
        48 b_u3 49 b_ur1""",
    "dve": """1 c_x2 2 c_u4 6 c_u5 6 c_x3 8 b_silu 9 c_ur2 9 b_tsg 13 b_xn 14 c_u6 14 c_u7 16 c_ur3 16 r_scan 20 a_norm
        21 b_q 22 a_xn 22 b_qs 23 c_fin 23 b_k 24 b_ks 24 b_v 26 c_out 27 b_ksum 30 a_logits 30 b_s02 31 b_s3
        32 b_s1 32 a_gate 32 b_pn 33 r_room 33 r_fin 37 b_pt0 39 b_pt1 40 b_x0 40 b_pt2 43 b_u0 43 b_u1 44 b_pv
        44 b_x1 45 b_ur0 48 b_u2 50 b_u3 50 b_ur1""",
    "pool": """10 b_tsg 17 b_xt 18 a_norm 21 b_qsum 24 a_xt 26 b_qlo 26 b_ksum 28 b_klo 29 b_hlo0 33 b_hlo1 44 b_pv""",
    "sp": """5 m_g2 17 a_load 21 m_g3 22 m_g4 26 c_out 26 b_gt 29 m_g5 30 m_g6 31 b_g0 32 b_g1 35 b_g2 38 m_g7 40 b_g3
        42 b_g4 44 b_g5 45 a_gt 46 a_g0 47 a_g1 48 b_g6 48 b_g7""",
    "pe_first": """8 r_up 24 a_xt 34 a_logits 41 a_gt""",
    "act_first": """1 w_s2 5 w_s3 7 w_s4 9 r_up 21 w_s5 22 a_xt 23 w_s6 31 w_s7 33 a_exp 35 w_s8 35 r_exp 38 r_root 41 a_gt
        41 w_s9 43 w_s10 52 w_s11""",
    "dve_first": """0 w_s2 4 w_s3 10 w_s4 12 r_scan 19 w_s5 20 a_norm 22 a_xn 22 w_s6 30 a_logits 32 w_s7 33 a_gate 33 r_room
        38 r_fin 38 w_s8 40 w_s9 44 w_s10 51 w_s11""",
    "pool_first": """19 a_norm 22 a_xt 30 w_c0 35 w_c1 39 w_c2 48 w_c3""",
    "sp_first": """5 w_l6 6 m_g2 7 w_l7 11 w_l8 12 w_l9 12 w_rope 15 w_l10 16 m_g3 20 a_load 21 m_g4 22 w_l11 23 w_l12
        24 m_g5 25 w_l13 25 m_g6 31 w_l14 39 a_gt 39 m_g7 40 w_l15 41 a_g0 48 a_g1""",
    "pe_last": """4 c_u4 6 c_u5 6 c_ur2 9 b_tsg 13 c_d2 14 c_u6 15 c_u7 16 b_xt 28 c_ur3 29 c_d3 30 b_q 32 b_qs 34 b_k
        35 b_route 35 b_ks 37 b_v 38 c_out 39 b_su0 39 b_su1 40 b_s02 45 b_s3 50 b_s1 53 b_gt 53 b_sd 53 b_pt0
        53 b_pt1 53 b_pt2 53 b_u0 53 b_u1 53 b_pv 53 b_ur0 53 b_d0 53 b_o 53 b_u2 53 b_u3 53 b_ur1 53 b_d1""",
    "act_last": """3 c_u4 6 c_u5 8 b_silu 10 c_ur2 13 c_u6 13 c_u7 15 c_ur3 27 b_xt 28 c_fin 34 b_qsum 36 b_route 37 b_v
        37 b_ksum 39 b_su0 47 b_su1 48 b_sq0 49 b_hhi0 50 b_sq1 53 b_prob 53 b_hhi1 53 b_gt 53 b_pt0 53 b_pt1
        53 b_pt2 53 b_u0 53 b_u1 53 b_pv 53 b_ur0 53 b_o 53 b_u2 53 b_u3 53 b_ur1""",
    "dve_last": """1 c_x2 5 c_u4 6 c_u5 6 c_x3 6 b_silu 7 c_ur2 10 b_tsg 13 c_u6 15 c_u7 20 b_xn 23 c_ur3 30 b_q 32 b_qs
        32 b_k 32 b_ks 36 c_fin 37 b_v 38 c_out 38 b_ksum 39 b_s02 44 b_s3 50 b_s1 53 b_pn 53 b_pt0 53 b_pt1
        53 b_x0 53 b_pt2 53 b_u0 53 b_u1 53 b_pv 53 b_x1 53 b_ur0 53 b_u2 53 b_u3 53 b_ur1""",
    "pool_last": """5 b_tsg 26 b_xt 27 b_qsum 37 b_qlo 38 b_ksum 40 b_klo 48 b_hlo0 53 b_hlo1 53 b_pv""",
    "sp_last": """31 b_gt 32 c_out 39 b_g0 50 b_g1 53 b_g2 53 b_g3 53 b_g4 53 b_g5 53 b_g6 53 b_g7""",
}
RING0, RING1 = 2, 4
LAG = 3
SLOTS = 4
WHOLE = 3
MULTIPLY_PART, GATE_PART, ROUND_PART, LO_PART_DVE, LO_PART_POOL = 0, 0, 1, 1, 2
LO_DVE = {3, 7, 9, 14, 16}


class At:

    def __init__(self, n, parity=None):
        self.n = n
        self.parity = n % 2 if parity is None else parity

    def __add__(self, k):
        return At(self.n + k, (self.parity + k) % 2)

    def batch(self, step):
        return self + {"a": 1, "m": 0, "r": 0, "b": -1, "c": -2, "w": 0}[step[0]]

    def has(self, stage):
        if stage == "w":
            return isinstance(self.n, int) and self.n == 0
        if not isinstance(self.n, int):
            return True
        return {"a": -1 <= self.n < NB - 1, "m": 0 <= self.n < NB, "r": self.n < NB,
                "b": 0 < self.n <= NB, "c": self.n > 1}[stage]


def steps(engine, i, h, part):
    first_or_last = "" if not isinstance(i.n, int) else "_first" if i.n == 0 else "_last" if i.n >= NB else ""
    words = SCHEDULE[engine + first_or_last].split()
    return [s for at, s in zip(words[::2], words[1::2]) if int(at) == 3 * h + part and i.has(s[0])]


def order(i, way_up):
    out = []
    for h in range(NH):
        for part in range(3):
            if i.has("m") and part == way_up:
                out.append(("up", h))
            out += steps("pe", i, h, part)
    return out


def slot(i, h):
    return (NH * i.parity + h) % SLOTS


def lo_count(h):
    return sum((k in LO_DVE) == (h in LO_DVE) for k in range(h + 1))


def hidden_before(i, h, distance):
    return (i, h - distance) if h >= distance else (i + -1, h - distance + NH)


class Ring:

    LEAD = ["a_xt", "a_logits", "a_gt"]

    def __init__(self, full, banks, uses, way_up=None):
        self.full, self.banks, self.uses, self.way_up = full, banks, uses, way_up
        self.read = {}
        self.length = len(self._of(At(2)))
        assert self.length % 2 == 0

    def _of(self, i):
        return [u for u in order(i, self.way_up) if (u if isinstance(u, str) else u[0]) in self.uses]

    def _until(self, n):
        users = [(u, At(-1)) for u in self.LEAD if u in self.uses]
        for k in range(n):
            users += [(u, At(k)) for u in self._of(At(k))]
        return users

    def number(self, i, user):
        if i.n == -1 if isinstance(i.n, int) else False:
            return [u for u, _ in self._until(0)].index(user), 0
        if isinstance(i.n, int):
            return len(self._until(i.n)) + self._of(i).index(user), 0
        return len(self._until(2)) - 2 * self.length + self._of(At(2)).index(user), self.length

    def bank(self, i, user):
        return self.banks[self.number(i, user)[0] % 2]

    def filled(self, i, user):
        n, per = self.number(i, user)
        return per * i.n + (n + 1) if per else n + 1

    def previous(self, i, user):
        if isinstance(i.n, int):
            n = self.number(i, user)[0]
            return (self._until(i.n + 1))[n - 2] if n >= 2 else None
        users = self._of(At(2))
        at = users.index(user) - 2
        return (users[at], i) if at >= 0 else (users[at], i + -1)


def build_layers(nc, x, weights, weights16, columns, rope, masks, rank_ties, expert_bias, out):
    F32, F32R, BF16 = mybir.dt.float32, mybir.dt.float32r, mybir.dt.bfloat16
    ALU, ACT, AX = mybir.AluOpType, mybir.ActivationFunctionType, mybir.AxisListType
    SCALE = float(P) ** -0.5

    with ExitStack() as ctx:
        def sb(name, shape, dt=F32):
            return ctx.enter_context(nc.sbuf_tensor(name, shape, dt))

        def sem(name):
            return ctx.enter_context(nc.semaphore(name))

        def bank(name):
            return ctx.enter_context(nc.psum_tensor(name, [P, T], F32))

        w_hi = sb("w_hi", [P, W_ALL], F32R)
        w_lo = sb("w_lo", [P, W_ALL], F32R)
        w16 = sb("w16", [P, V_ALL], BF16)
        cols = sb("cols", [P, C_N])
        cos_sin = sb("cos_sin", [P, 2, T])
        const = sb("const", [P, 2, P])
        ident, causal = const[:, 0, :], const[:, 1, :]
        ties = sb("ties", [P, E, E])
        bias8 = sb("bias8", [P, E])
        ln_floor = sb("ln_floor", [P, 1])
        minus_half = sb("minus_half", [P, NT])
        half_bias = sb("half_bias", [P, 2])
        decay = sb("decay", [P, 6])
        x_in = sb("x_in", [P, 2, NT, P])
        stats0 = sb("stats0", [P, NT, 6])
        mv0 = sb("mv0", [P, NT, 2])
        var0 = sb("var0", [P, NT])
        rstd0 = sb("rstd0", [P, NT])
        xn0 = sb("xn0", [P, NT, P])
        xn1 = xn0
        x0t = sb("x0t", [P, T])
        x0_hi = sb("x0_hi", [P, 2, T], F32R)
        x0_lo = sb("x0_lo", [P, 2, T], F32R)
        logit = sb("logit", [P, NT, E])
        top = sb("top", [P, NT, 4])
        score0 = sb("score0", [P, NT, E])
        beats = sb("beats", [P, NT, E, E])
        rank = sb("rank", [P, NT, E])
        gate0 = sb("gate0", [P, NT, E])
        gate0_t = sb("gate0_t", [E, T])
        gates0 = sb("gates0", [P, RING0, T])
        silu = sb("silu", [P, 2, T])
        hid_hi = sb("hid_hi", [P, SLOTS, T], F32R)
        hid_lo = sb("hid_lo", [P, SLOTS, T], F32R)
        hid = sb("hid", [P, WHOLE, T])
        tanh_x = sb("tanh_x", [P, T])
        tanh_a = sb("tanh_a", [P, T])
        log_a = tanh_a
        level = sb("level", [P, T])
        step_a = sb("step_a", [P, T])
        sq = level
        normed = tanh_x
        state = sb("state", [P, T])
        ctxt = sb("ctxt", [P, T])
        g0 = ctxt
        sg0 = g0
        x1 = sb("x1", [P, 2, NT, P])
        stats1 = sb("stats1", [P, NT, 6])
        mv1 = sb("mv1", [P, NT, 2])
        var1 = sb("var1", [P, NT])
        rstd1 = sb("rstd1", [P, NT])
        x1t = sb("x1t", [P, 2, T])
        x1_hi = sb("x1_hi", [P, T], F32R)
        x1_lo = sb("x1_lo", [P, T], F32R)
        rot = sb("rot", [P, 4, T])
        pt_hi = sb("pt_hi", [P, 3, T], F32R)
        pt_lo = sb("pt_lo", [P, 3, T], F32R)
        q_hi, q_lo, k_hi, k_lo = pt_hi[:, 0], pt_lo[:, 0], pt_hi[:, 1], pt_lo[:, 1]
        v_hi = sb("v_hi", [P, T], F32R)
        v_lo = sb("v_lo", [P, T], F32R)
        top1 = sb("top1", [P, 4 * NT])
        smax, nmax, ssum, rsum = (top1[:, NT * n:NT * (n + 1)] for n in range(4))
        prob = sb("prob", [P, NT * (NT + 1) // 2 * P])
        ctx_hi, ctx_lo = x1_hi, x1_lo
        attn = sb("attn", [P, T])
        tanh1 = sb("tanh1", [P, NT, E])
        score1 = sb("score1", [P, NT, E])
        biased = sb("biased", [P, NT, E])
        beats1 = beats
        rank1 = sb("rank1", [P, NT, E])
        gate1 = sb("gate1", [P, NT, E])
        gate1_t = sb("gate1_t", [E, T])
        gates1 = sb("gates1", [P, RING1, T])
        hs = sb("hs", [P, 2, T])
        hs1 = sb("hs1", [P, 2, T], F32R)
        hs_hi = [pt_hi[:, 2], hs1[:, 0]]
        hs_lo = [pt_lo[:, 2], hs1[:, 1]]
        routed_in = sb("routed_in", [P, 4, T], BF16)
        prob16 = prob[:].bitcast(BF16).rearrange("p (k t) -> p k t", t=T)
        hs16 = hs[:].rearrange("p k t -> p (k t)").bitcast(BF16).rearrange("p (k t) -> p k t", t=T)
        hid16 = [*(prob16[:, k] for k in range(5)), hs16[:, 2]]
        relu16 = [hs16[:, 0], hs16[:, 1]]
        g1 = hs[:, 0]
        sg1 = g1
        y_out = x1
        stages = [hs[:].rearrange("p k t -> p (k t)"), prob[:]]
        stages += [rot[:].rearrange("p (s k) t -> p s (k t)", s=2)[:, k] for k in range(2)]
        stages += [gates1[:].rearrange("p (s k) t -> p s (k t)", s=2)[:, k] for k in range(2)]
        w_stage = [stages[c % len(stages)] for c in range(W_CHUNKS + V_CHUNKS)]
        w16_stage = [stage[:, 0:V_CHUNK] for stage in w_stage[W_CHUNKS:]]

        gate0_dram = nc.dram_tensor("gate0_scratch", [2, E * T], F32).ap()
        gate1_dram = nc.dram_tensor("gate1_scratch", [2, E * T], F32).ap()

        G = Ring(sem("g_full"), [bank("g_even"), bank("g_odd")], ("up", "b_tsg", "r_up", "a_xt", "a_gt"), way_up=0)
        U = Ring(sem("u_full"), [bank("u_even"), bank("u_odd")], ("up", "r_up", "a_logits"), way_up=1)
        PAIR = [[f"{stage}_u{2 * p}", f"{stage}_u{2 * p + 1}", f"{stage}_ur{p}"] for p, stage in enumerate("bbcc")]
        B_USES = ("b_xt", "b_q", "b_qs", "b_k", "b_ks", "b_route", "b_v", "b_su0", "b_su1", "b_s02", "b_s3",
                  "b_gt", "b_pt0", "b_pt1", "b_pt2", "b_pv", "b_o", "c_out",
                  *(user for users in PAIR for user in users))
        Z = Ring(sem("z_full"), [bank("z_even"), bank("z_odd")], B_USES)
        y0 = bank("y0")
        y1 = bank("y1")

        w_in = [sem(f"w_in_{c}") for c in range(W_CHUNKS)]
        w16_in = [sem(f"w16_in_{c}") for c in range(V_CHUNKS)]
        cols_in, rope_in, const_in, ties_in, bias8_in = (
            sem(n) for n in ("cols_in", "rope_in", "const_in", "ties_in", "bias8_in"))
        w_rounded, w_split, w16_cast, const_set, half_set = (
            sem(n) for n in ("w_rounded", "w_split", "w16_cast", "const_set", "half_set"))
        soft_dve, soft_act = sem("soft_dve"), sem("soft_act")

        counts = {}

        def signal(name, per):
            s = sem(name)
            counts[id(s)] = per
            return s

        passed_sp, passed_dve = sem("passed_sp"), sem("passed_dve")

        def upto(s, b, k):
            value = counts[id(s)] * b.n + k
            return max(value, 0) if isinstance(value, int) else value

        def emptied(ring, i, user):
            before = ring.previous(i, user)
            if before is None:
                return ring.full, 0
            last, at = before
            s, k = ring.read[last]
            return s, upto(s, at.batch("m" if isinstance(last, tuple) else last), k)

        def view(ring, i, user):
            return ring.bank(i, user)

        x_loaded = [signal("x_loaded_even", 8), signal("x_loaded_odd", 8)]
        stats0_done = signal("stats0_done", NT)
        mv0_done = signal("mv0_done", NT)
        var0_done = signal("var0_done", 1)
        rstd0_done = signal("rstd0_done", 1)
        xn0_done = signal("xn0_done", NT)
        x0t_done = signal("x0t_done", 1)
        x0_hi_done = signal("x0_hi_done", 1)
        x0_lo_done = signal("x0_lo_done", 1)
        router0 = signal("router0", 13)
        exp0_done = signal("exp0_done", 1)
        gate0_t_done = signal("gate0_t_done", 1)
        gate0_stored = signal("gate0_stored", 16)
        gates0_in = [signal(f"gates0_in_{r}", 16 * E // RING0) for r in range(RING0)]
        silu_done = signal("silu_done", NH)
        mul_done = signal("mul_done", NH)
        gated_done = signal("gated_done", NH - 2)
        hi_done = signal("hi_done", NH)
        lo_dve = signal("lo_dve", len(LO_DVE))
        lo_pool = signal("lo_pool", NH - len(LO_DVE))
        down_done = signal("down_done", NH)
        tanh_done = signal("tanh_done", 2)
        log_a_done = signal("log_a_done", 1)
        level_done = signal("level_done", 2)
        step_done = signal("step_done", 2)
        a2_done = signal("a2_done", 1)
        ratio_done = signal("ratio_done", 1)
        room_done = signal("room_done", 1)
        root_done = signal("root_done", 1)
        gated_x_done = signal("gated_x_done", 1)
        normed_done = signal("normed_done", 1)
        state_done = signal("state_done", 1)
        g0_done = signal("g0_done", 1)
        sg0_done = signal("sg0_done", 1)
        x1_done = signal("x1_done", 1)
        stats1_done = signal("stats1_done", NT)
        mv1_done = signal("mv1_done", NT)
        var1_done = signal("var1_done", 1)
        rstd1_done = signal("rstd1_done", 1)
        xn1_done = signal("xn1_done", NT)
        x1t_done = signal("x1t_done", 1)
        x1_hi_done = signal("x1_hi_done", 1)
        x1_lo_done = signal("x1_lo_done", 1)
        x1_used = signal("x1_used", 1)
        rot_done = signal("rot_done", 4)
        qk_done = signal("qk_done", 2)
        qk_hi_done = signal("qk_hi_done", 2)
        qk_lo_done = signal("qk_lo_done", 2)
        v_hi_done = signal("v_hi_done", 1)
        v_lo_done = signal("v_lo_done", 1)
        tanh1_done = signal("tanh1_done", 1)
        router1 = signal("router1", 6)
        gate1_t_done = signal("gate1_t_done", 1)
        gate1_stored = signal("gate1_stored", 16)
        gates1_in = [signal(f"gates1_in_{r}", 16 * E // RING1) for r in range(RING1)]
        s1_full = signal("s1_full", 1)
        scores_done = signal("scores_done", 1)
        masked_done = signal("masked_done", NT)
        max_done = signal("max_done", NT)
        nmax_done = signal("nmax_done", 1)
        prob_done = signal("prob_done", NT)
        rsum_done = signal("rsum_done", 1)
        prob_normed = signal("prob_normed", NT)
        pt_hi_done = signal("pt_hi_done", 3)
        pt_lo_done = signal("pt_lo_done", 3)
        pv_done = signal("pv_done", 1)
        ctx_done = signal("ctx_done", 1)
        ctx_hi_done = signal("ctx_hi_done", 1)
        ctx_lo_done = signal("ctx_lo_done", 1)
        attn_done = signal("attn_done", 1)
        hs_relu_done = signal("hs_relu_done", 2)
        hs_done = signal("hs_done", 2)
        hs_hi_done = signal("hs_hi_done", 2)
        hs_lo_done = signal("hs_lo_done", 2)
        shared_down = signal("shared_down", 1)
        routed_in_done = signal("routed_in_done", E)
        relu16_done = signal("relu16_done", 12)
        hid16_done = signal("hid16_done", 12)
        pair_down = signal("pair_down", E // 2)
        g1_done = signal("g1_done", 1)
        sg1_done = signal("sg1_done", 1)
        y_done = signal("y_done", 1)
        y_stored = signal("y_stored", 16)

        for h in range(NH):
            G.read["up", h] = (silu_done, h + 1)
            U.read["up", h] = (mul_done, h + 1)
        G.read.update(b_tsg=(x1_done, 1), r_up=(tanh_done, 1), a_xt=(x0_hi_done, 1), a_gt=(gate0_t_done, 1))
        U.read.update(r_up=(tanh_done, 2), a_logits=(router0, 2))
        Z.read.update(b_xt=(x1_hi_done, 1), b_q=(rot_done, 1), b_qs=(rot_done, 2), b_k=(rot_done, 3),
                      b_ks=(rot_done, 4), b_route=(tanh1_done, 1), b_v=(v_lo_done, 1), b_su0=(hs_relu_done, 1),
                      b_su1=(hs_relu_done, 2), b_s02=(prob_done, 3), b_s3=(prob_done, 4), b_gt=(gate1_t_done, 1),
                      b_pt0=(pt_lo_done, 1), b_pt1=(pt_lo_done, 2), b_pt2=(pt_lo_done, 3), b_pv=(ctx_done, 1),
                      b_o=(attn_done, 1), c_out=(y_done, 1))
        for p in range(E // 2):
            for k, user in enumerate(PAIR[p]):
                Z.read[user] = (relu16_done, 3 * p + k + 1)

        def split_matmul(o, w, rhs_hi, rhs_lo, start, stop):
            nc.tensor.matmul(o, w[0], rhs_hi, start=start, stop=False)
            nc.tensor.matmul(o, w[0], rhs_lo, start=False, stop=False)
            return nc.tensor.matmul(o, w[1], rhs_hi, start=False, stop=stop)

        def weight(c, n=P):
            return w_hi[:, c:c + n], w_lo[:, c:c + n]

        def tok(n, m=1):
            return slice(n * P, (n + m) * P)

        def iterations(eng, run):
            run(At(0))
            run(At(1))
            with eng.Fori(1, NB // 2 - 1) as j:
                run(At(2 * j, 0))
                run(At(2 * j + 1, 1))
            run(At(NB - 2))
            run(At(NB - 1))
            run(At(NB))
            run(At(NB + 1))

        PROB = {t: slice(t * (t + 1) // 2 * P, (t + 1) * (t + 2) // 2 * P) for t in range(NT)}
        PT_AT = {0: (0, 0), 1: (1, 0), 3: (1, 3 * P), 2: (2, 0)}
        PT_OF = [[0], [1, 3], [2]]

        def score_bank(i, t):
            if t == 1:
                return y1[:, tok(0, 2)]
            if t == 3:
                return view(Z, i, "b_s3")[:, :]
            return view(Z, i, "b_s02")[:, tok(0) if t == 0 else tok(1, 3)]

        block = ctx.enter_context(nc.Block())

        @block.sync
        def _(sp):
            def load_x(b):
                rows = x[b.n:b.n + 1].rearrange("b (n p) d -> p (b n) d", p=P)
                sp.dma_start(x_in[:, b.parity], rows).then_inc(x_loaded[b.parity], 16)

            load_x(At(0))
            sp.dma_start(const[:], masks).then_inc(const_in, 16)
            def load_weights(c):
                before = c - len(stages)
                if before >= W_CHUNKS:
                    sp.wait_ge(w16_cast, before - W_CHUNKS + 1)
                elif before >= 0:
                    sp.wait_ge(w_split, before + 1)
                if c >= W_CHUNKS:
                    v = c - W_CHUNKS
                    sp.dma_start(w_stage[c][:, 0:V_CHUNK], weights16[:, v * V_CHUNK:(v + 1) * V_CHUNK]).then_inc(w16_in[v], 16)
                else:
                    lo, hi = W_BOUNDS[c:c + 2]
                    sp.dma_start(w_stage[c][:, 0:hi - lo], weights[:, lo:hi]).then_inc(w_in[c], 16)

            for c in range(len(stages)):
                load_weights(c)
                if c == 0:
                    sp.dma_start(cols[:], columns).then_inc(cols_in, 16)
                    sp.dma_start(ties[:].rearrange("p a b -> p (a b)"), rank_ties).then_inc(ties_in, 16)
                    sp.dma_start(bias8[:], expert_bias.partition_broadcast(P)).then_inc(bias8_in, 16)
            def a_gt(i, b):
                sp.wait_ge(gate0_t_done, upto(gate0_t_done, b, 1))
                sp.dma_start(gate0_dram[b.parity].rearrange("(e t) -> e t", e=E), gate0_t[:]).then_inc(gate0_stored, 16)

            def spread0(e, at):
                def step(i, b):
                    sp.wait_ge(gated_done, upto(gated_done, b, 2 * (e - RING0) + 2))
                    if e == 0:
                        sp.sem_inc(passed_sp, 1)
                        sp.wait_ge(gate0_stored, upto(gate0_stored, b, 16))
                    sp.dma_start(gates0[:, e % RING0], gate0_dram[b.parity, e * T:(e + 1) * T].partition_broadcast(P)
                                 ).then_inc(gates0_in[e % RING0], 16)
                return step

            def b_gt(i, b):
                sp.wait_ge(gate1_t_done, upto(gate1_t_done, b, 1))
                sp.dma_start(gate1_dram[b.parity].rearrange("(e t) -> e t", e=E), gate1_t[:]).then_inc(gate1_stored, 16)

            def spread1(e):
                def step(i, b):
                    sp.wait_ge(routed_in_done, upto(routed_in_done, b, e - RING1 + 1))
                    if e == 0:
                        sp.sem_inc(passed_sp, 1)
                        sp.wait_ge(gate1_stored, upto(gate1_stored, b, 16))
                    sp.dma_start(gates1[:, e % RING1], gate1_dram[b.parity, e * T:(e + 1) * T].partition_broadcast(P)
                                 ).then_inc(gates1_in[e % RING1], 16)
                return step

            def a_load(i, b):
                row = b.n if isinstance(b.n, int) else sp.snap(b.n)
                sp.wait_ge(x1_done, upto(x1_done, b + -1, 0))
                sp.dma_start(x_in[:, b.parity], x[bass.ds(row, 1)].rearrange("b (n p) d -> p (b n) d", p=P)
                             ).then_inc(x_loaded[b.parity], 16)

            def c_out(i, b):
                row = b.n if isinstance(b.n, int) else sp.snap(b.n)
                sp.wait_ge(y_done, upto(y_done, b, 1))
                sp.dma_start(out[bass.ds(row, 1)].rearrange("b (n p) d -> p (b n) d", p=P), y_out[:, b.parity]
                             ).then_inc(y_stored, 16)

            def w_rope(i, b):
                sp.dma_start(cos_sin[:], rope).then_inc(rope_in, 16)

            STEPS = {"a_load": a_load, "a_gt": a_gt, "b_gt": b_gt, "c_out": c_out, "w_rope": w_rope}
            for c in range(len(stages), W_CHUNKS + V_CHUNKS):
                STEPS[f"w_l{c}"] = lambda i, b, c=c: load_weights(c)
            for e in range(E):
                STEPS[f"a_g{e}" if e < RING0 else f"m_g{e}"] = spread0(e, 0)
                STEPS[f"b_g{e}"] = spread1(e)

            a_gt(At(-1), At(0))
            for e in range(RING0):
                STEPS[f"a_g{e}"](At(-1), At(0))

            def run(i):
                for h in range(NH):
                    for part in range(3):
                        for s in steps("sp", i, h, part):
                            STEPS[s](i, i.batch(s))
                if i.has("w"):
                    sp.wait_ge(w16_cast, V_CHUNKS)

            iterations(sp, run)
            sp.wait_ge(y_stored, 16 * NB)

        @block.tensor
        def _(pe):
            def a_xt(i, b):
                g = view(G, i, "a_xt")
                pe.wait_ge(*emptied(G, i, "a_xt"))
                pe.wait_ge(xn0_done, upto(xn0_done, b, NT))
                for n in range(NT):
                    last = nc.tensor.transpose(g[:, tok(n)], xn0[:, n, :], ident)
                last.then_inc(G.full, 1)

            def a_logits(i, b):
                u = view(U, i, "a_logits")
                pe.wait_ge(*emptied(U, i, "a_logits"))
                pe.wait_ge(x0_lo_done, upto(x0_lo_done, b, 1))
                w = weight(W_ROUTE0, E)
                for n in range(NT):
                    xh, xl = (x0[:, b.parity, tok(n)] for x0 in (x0_hi, x0_lo))
                    o = u[:, n * E:(n + 1) * E]
                    nc.tensor.matmul(o, xh, w[0], start=True, stop=False)
                    nc.tensor.matmul(o, xh, w[1], start=False, stop=False)
                    last = nc.tensor.matmul(o, xl, w[0], start=False, stop=True)
                last.then_inc(U.full, 1)

            def a_gt(i, b):
                g = view(G, i, "a_gt")
                pe.wait_ge(*emptied(G, i, "a_gt"))
                pe.wait_ge(router0, upto(router0, b, 13))
                for n in range(NT):
                    last = nc.tensor.transpose(g[0:E, tok(n)], gate0[:, n, :], ident)
                last.then_inc(G.full, 1)

            def r_up(i, b):
                g = view(G, i, "r_up")
                pe.wait_ge(*emptied(G, i, "r_up"))
                u = view(U, i, "r_up")
                pe.wait_ge(*emptied(U, i, "r_up"))
                xh, xl = x0_hi[:, b.parity], x0_lo[:, b.parity]
                split_matmul(g[:], weight(W_IG), xh, xl, True, True).then_inc(G.full, 1)
                split_matmul(u[:], weight(W_AG), xh, xl, True, True).then_inc(U.full, 1)

            def b_tsg(i, b):
                g = view(G, i, "b_tsg")
                pe.wait_ge(*emptied(G, i, "b_tsg"))
                pe.wait_ge(sg0_done, upto(sg0_done, b, 1))
                for n in range(NT):
                    last = nc.tensor.transpose(g[:, tok(n)], sg0[:, tok(n)], ident)
                last.then_inc(G.full, 1)

            def b_xt(i, b):
                z = view(Z, i, "b_xt")
                pe.wait_ge(*emptied(Z, i, "b_xt"))
                pe.wait_ge(xn1_done, upto(xn1_done, b, NT))
                for n in range(NT):
                    last = nc.tensor.transpose(z[:, tok(n)], xn1[:, n, :], ident)
                last.then_inc(Z.full, 1)

            def project(name, column):
                def step(i, b):
                    z = view(Z, i, name)
                    pe.wait_ge(*emptied(Z, i, name))
                    if name == "b_q":
                        pe.wait_ge(x1_lo_done, upto(x1_lo_done, b, 1))
                    split_matmul(z[:], weight(column), x1_hi[:], x1_lo[:], True, True).then_inc(Z.full, 1)
                return step

            def b_route(i, b):
                z = view(Z, i, "b_route")
                pe.wait_ge(*emptied(Z, i, "b_route"))
                w = weight(W_ROUTE1, E)
                for n in range(NT):
                    o = z[:, n * E:(n + 1) * E]
                    nc.tensor.matmul(o, x1_hi[:, tok(n)], w[0], start=True, stop=False)
                    nc.tensor.matmul(o, x1_hi[:, tok(n)], w[1], start=False, stop=False)
                    last = nc.tensor.matmul(o, x1_lo[:, tok(n)], w[0], start=False, stop=True)
                last.then_inc(Z.full, 1)

            def b_v(i, b):
                z = view(Z, i, "b_v")
                pe.wait_ge(*emptied(Z, i, "b_v"))
                w = weight(W_V)
                for n in range(NT):
                    o = z[:, tok(n)]
                    nc.tensor.matmul(o, x1_hi[:, tok(n)], w[0], start=True, stop=False)
                    nc.tensor.matmul(o, x1_hi[:, tok(n)], w[1], start=False, stop=False)
                    last = nc.tensor.matmul(o, x1_lo[:, tok(n)], w[0], start=False, stop=True)
                last.then_inc(Z.full, 1)

            def shared_up(j):
                def step(i, b):
                    z = view(Z, i, f"b_su{j}")
                    pe.wait_ge(*emptied(Z, i, f"b_su{j}"))
                    last = split_matmul(z[:], weight(W_SU + j * P), x1_hi[:], x1_lo[:], True, True)
                    last.then_inc(Z.full, 1)
                return step

            def scores_of(o, t):
                q = (q_hi[:, tok(t)], q_lo[:, tok(t)])
                return split_matmul(o, q, k_hi[:, tok(0, t + 1)], k_lo[:, tok(0, t + 1)], True, True)

            def b_s02(i, b):
                pe.wait_ge(*emptied(Z, i, "b_s02"))
                pe.wait_ge(qk_lo_done, upto(qk_lo_done, b, 2))
                scores_of(score_bank(i, 0), 0)
                scores_of(score_bank(i, 2), 2).then_inc(Z.full, 1)

            def b_s3(i, b):
                pe.wait_ge(*emptied(Z, i, "b_s3"))
                scores_of(score_bank(i, 3), 3).then_inc(Z.full, 1)

            def b_s1(i, b):
                pe.wait_ge(g1_done, upto(g1_done, b, 0))
                scores_of(score_bank(i, 1), 1).then_inc(s1_full, 1)

            def b_gt(i, b):
                z = view(Z, i, "b_gt")
                pe.wait_ge(*emptied(Z, i, "b_gt"))
                pe.wait_ge(router1, upto(router1, b, 6))
                for n in range(NT):
                    last = nc.tensor.transpose(z[0:E, tok(n)], gate1[:, n, :], ident)
                last.then_inc(Z.full, 1)

            def b_sd(i, b):
                pe.wait_ge(prob_done, upto(prob_done, b, NT))
                for j in range(2):
                    pe.wait_ge(hs_lo_done, upto(hs_lo_done, b, j + 1))
                    last = split_matmul(y1[:], weight(W_SD + j * P), hs_hi[j], hs_lo[j], j == 0, False)
                last.then_inc(shared_down, 1)

            def transposed_probs(m):
                def step(i, b):
                    z = view(Z, i, f"b_pt{m}")
                    pe.wait_ge(*emptied(Z, i, f"b_pt{m}"))
                    pe.wait_ge(prob_normed, upto(prob_normed, b, NT))
                    for s in PT_OF[m]:
                        at = PT_AT[s][1]
                        for t in range(s, NT):
                            src = prob[:, PROB[t].start + s * P:PROB[t].start + (s + 1) * P]
                            last = nc.tensor.transpose(z[:, at + (t - s) * P:at + (t - s + 1) * P], src, ident)
                    last.then_inc(Z.full, 1)
                return step

            def b_pv(i, b):
                z = view(Z, i, "b_pv")
                pe.wait_ge(*emptied(Z, i, "b_pv"))
                pe.wait_ge(v_lo_done, upto(v_lo_done, b, 1))
                pe.wait_ge(pt_lo_done, upto(pt_lo_done, b, 3))
                for s in range(NT):
                    m, at = PT_AT[s]
                    n = (NT - s) * P
                    v = (v_hi[:, tok(s)], v_lo[:, tok(s)])
                    last = split_matmul(z[:, s * P:T], v, pt_hi[:, m, at:at + n], pt_lo[:, m, at:at + n],
                                        s == 0, s == NT - 1)
                last.then_inc(Z.full, 1)

            def b_o(i, b):
                z = view(Z, i, "b_o")
                pe.wait_ge(*emptied(Z, i, "b_o"))
                pe.wait_ge(ctx_lo_done, upto(ctx_lo_done, b, 1))
                split_matmul(z[:], weight(W_O), ctx_hi[:], ctx_lo[:], True, True).then_inc(Z.full, 1)

            def routed_up(e):
                name = PAIR[e // 2][e % 2]

                def step(i, b):
                    z = view(Z, i, name)
                    pe.wait_ge(*emptied(Z, i, name))
                    pe.wait_ge(routed_in_done, upto(routed_in_done, b, e + 1))
                    nc.tensor.matmul(z[:], w16[:, V_U + e * P:V_U + (e + 1) * P], routed_in[:, e % 4],
                                     start=True, stop=True).then_inc(Z.full, 1)
                return step

            def routed_up_rest(p):
                name = PAIR[p][2]

                def step(i, b):
                    z = view(Z, i, name)
                    pe.wait_ge(*emptied(Z, i, name))
                    for k in range(2):
                        c = V_UR + p * P + k * HALF
                        last = nc.tensor.matmul(z[k * HALF:(k + 1) * HALF, :], w16[:, c:c + HALF],
                                                routed_in[:, (2 * p + k) % 4], start=True, stop=True)
                    last.then_inc(Z.full, 1)
                return step

            def routed_down(p):
                def step(i, b):
                    pe.wait_ge(hid16_done, upto(hid16_done, b, 3 * p + 3))
                    for k, c in enumerate((V_D + 2 * p * P, V_D + (2 * p + 1) * P, V_DR + p * P)):
                        last = nc.tensor.matmul(y1[:], w16[:, c:c + P], hid16[(3 * p + k) % 6],
                                                start=False, stop=(p == E // 2 - 1 and k == 2))
                    last.then_inc(pair_down, 1)
                return step

            def c_out(i, b):
                z = view(Z, i, "c_out")
                pe.wait_ge(*emptied(Z, i, "c_out"))
                pe.wait_ge(sg1_done, upto(sg1_done, b, 1))
                for n in range(NT):
                    last = nc.tensor.transpose(z[:, tok(n)], sg1[:, tok(n)], ident)
                last.then_inc(Z.full, 1)

            STEPS = {"a_xt": a_xt, "a_logits": a_logits, "a_gt": a_gt, "r_up": r_up, "b_tsg": b_tsg, "b_xt": b_xt,
                     "b_q": project("b_q", W_Q), "b_qs": project("b_qs", W_QS), "b_k": project("b_k", W_K),
                     "b_ks": project("b_ks", W_KS), "b_route": b_route, "b_v": b_v, "b_su0": shared_up(0),
                     "b_su1": shared_up(1), "b_s02": b_s02, "b_s3": b_s3, "b_s1": b_s1, "b_gt": b_gt, "b_sd": b_sd,
                     "b_pt0": transposed_probs(0), "b_pt1": transposed_probs(1), "b_pt2": transposed_probs(2),
                     "b_pv": b_pv, "b_o": b_o, "c_out": c_out}
            for e in range(E):
                STEPS[PAIR[e // 2][e % 2]] = routed_up(e)
            for p in range(E // 2):
                STEPS[PAIR[p][2]] = routed_up_rest(p)
                STEPS["bbcc"[p] + f"_d{p}"] = routed_down(p)

            def up(i, h, which):
                ring = (G, U)[which]
                o = view(ring, i, ("up", h))
                pe.wait_ge(*emptied(ring, i, ("up", h)))
                if i.has("w"):
                    pe.wait_ge(w_split, h // 2 + 2)
                c = W_EXPERT + h // 2 * EXPERT + which * HID0 + h % 2 * P
                split_matmul(o[:], weight(c), x0_hi[:, i.parity], x0_lo[:, i.parity], True, True).then_inc(ring.full, 1)

            def down(i, h):
                if h == 0:
                    pe.wait_ge(g0_done, upto(g0_done, i, 0))
                r = slot(i, h)
                lo = lo_dve if h in LO_DVE else lo_pool
                pe.wait_ge(lo, upto(lo, i, lo_count(h)))
                c = W_EXPERT + h // 2 * EXPERT + 2 * HID0 + h % 2 * P
                split_matmul(y0[:], weight(c), hid_hi[:, r], hid_lo[:, r], h == 0,
                             h == NH - 1).then_inc(down_done, 1)

            def run(i):
                for h in range(NH):
                    for part in range(3):
                        if i.has("m") and part < 2:
                            up(i, h, part)
                        before = hidden_before(i, h, LAG)
                        if part == 2 and before[0].has("m"):
                            down(*before)
                        for s in steps("pe", i, h, part):
                            STEPS[s](i, i.batch(s))
                if i.has("w"):
                    pe.wait_ge(w_split, W_CHUNKS)
                    pe.wait_ge(w16_cast, V_CHUNKS)

            pe.wait_ge(const_in, 16)
            a_xt(At(-1), At(0))
            pe.wait_ge(w_split, 1)
            a_logits(At(-1), At(0))
            a_gt(At(-1), At(0))
            iterations(pe, run)

        @block.scalar
        def _(act):
            def a_xt(i, b):
                g = view(G, i, "a_xt")
                act.wait_ge(G.full, G.filled(i, "a_xt"))
                act.wait_ge(gated_x_done, upto(gated_x_done, b, 0))
                act.wait_ge(x0_lo_done, upto(x0_lo_done, b, 0))
                nc.scalar.copy(x0t[:], g[:]).then_inc(x0t_done, 1)
                act.wait_ge(down_done, upto(down_done, b + -1, 0))
                nc.scalar.copy(x0_hi[:, b.parity], g[:]).then_inc(x0_hi_done, 1)

            def a_exp(i, b):
                act.wait_ge(router0, upto(router0, b, 2))
                nc.scalar.activation(score0[:], logit[:], ACT.Exp).then_inc(exp0_done, 1)

            def a_gt(i, b):
                act.wait_ge(G.full, G.filled(i, "a_gt"))
                act.wait_ge(gate0_stored, upto(gate0_stored, b, 0))
                nc.scalar.copy(gate0_t[:], view(G, i, "a_gt")[0:E, :]).then_inc(gate0_t_done, 1)

            def r_up(i, b):
                act.wait_ge(G.full, G.filled(i, "r_up"))
                act.wait_ge(state_done, upto(state_done, b, 0))
                nc.scalar.activation(tanh_x[:], view(G, i, "r_up")[:], ACT.Tanh, bias=half_bias[:, 0:1],
                                     scale=0.5).then_inc(tanh_done, 1)
                act.wait_ge(U.full, U.filled(i, "r_up"))
                act.wait_ge(log_a_done, upto(log_a_done, b, 0))
                nc.scalar.activation(tanh_a[:], view(U, i, "r_up")[:], ACT.Tanh, bias=half_bias[:, 1:2],
                                     scale=0.5).then_inc(tanh_done, 1)

            def b_prob(i, b):
                act.wait_ge(nmax_done, upto(nmax_done, b, 1))
                act.wait_ge(prob_normed, upto(prob_normed, b, 0))
                act.wait_ge(pt_lo_done, upto(pt_lo_done, b, 0))
                for t in range(NT):
                    nc.scalar.activation(prob[:, PROB[t]], score_bank(i, t), ACT.Exp, bias=nmax[:, t:t + 1],
                                         scale=SCALE, accum_out=ssum[:, t:t + 1]).then_inc(prob_done, 1)

            def r_exp(i, b):
                act.wait_ge(log_a_done, upto(log_a_done, b, 1))
                act.wait_ge(normed_done, upto(normed_done, b, 0))
                act.wait_ge(step_done, upto(step_done, b, 2))
                nc.scalar.activation(sq[:], log_a[:], ACT.Exp, scale=2.0).then_inc(a2_done, 1)
                nc.scalar.activation(step_a[:], step_a[:], ACT.Exp).then_inc(ratio_done, 1)

            def r_root(i, b):
                act.wait_ge(room_done, upto(room_done, b, 1))
                nc.scalar.activation(sq[:], sq[:], ACT.Sqrt, scale=-0.25).then_inc(root_done, 1)

            def b_silu(i, b):
                act.wait_ge(down_done, upto(down_done, b, NH))
                act.wait_ge(sg0_done, upto(sg0_done, b, 0))
                nc.scalar.activation(g0[:], y0[:], ACT.Silu).then_inc(g0_done, 1)

            def b_xt(i, b):
                z = view(Z, i, "b_xt")
                act.wait_ge(Z.full, Z.filled(i, "b_xt"))
                act.wait_ge(routed_in_done, upto(routed_in_done, b + -1, 0))
                nc.scalar.copy(x1t[:, b.parity], z[:]).then_inc(x1t_done, 1)
                nc.scalar.copy(x1_hi[:], z[:]).then_inc(x1_hi_done, 1)

            def b_qsum(i, b):
                act.wait_ge(qk_done, upto(qk_done, b, 1))
                nc.scalar.copy(q_hi, rot[:, 0]).then_inc(qk_hi_done, 1)

            def b_ksum(i, b):
                act.wait_ge(qk_done, upto(qk_done, b, 2))
                nc.scalar.copy(k_hi, rot[:, 2]).then_inc(qk_hi_done, 1)

            def b_v(i, b):
                act.wait_ge(Z.full, Z.filled(i, "b_v"))
                nc.scalar.copy(v_hi[:], view(Z, i, "b_v")[:]).then_inc(v_hi_done, 1)

            def b_route(i, b):
                act.wait_ge(Z.full, Z.filled(i, "b_route"))
                z = view(Z, i, "b_route")[:, 0:NT * E].rearrange("p (n e) -> p n e", e=E)
                nc.scalar.activation(tanh1[:], z, ACT.Tanh, scale=0.5).then_inc(tanh1_done, 1)

            def shared_up(j):
                def step(i, b):
                    act.wait_ge(Z.full, Z.filled(i, f"b_su{j}"))
                    nc.scalar.activation(hs[:, j], view(Z, i, f"b_su{j}")[:], ACT.Relu).then_inc(hs_relu_done, 1)
                return step

            def squared(j):
                def step(i, b):
                    act.wait_ge(hs_relu_done, upto(hs_relu_done, b, j + 1))
                    nc.scalar.activation(hs[:, j], hs[:, j], ACT.Square).then_inc(hs_done, 1)
                return step

            def b_gt(i, b):
                act.wait_ge(Z.full, Z.filled(i, "b_gt"))
                act.wait_ge(gate1_stored, upto(gate1_stored, b, 0))
                nc.scalar.copy(gate1_t[:], view(Z, i, "b_gt")[0:E, :]).then_inc(gate1_t_done, 1)

            def round_shared(j):
                def step(i, b):
                    act.wait_ge(hs_done, upto(hs_done, b, j + 1))
                    nc.scalar.copy(hs_hi[j], hs[:, j]).then_inc(hs_hi_done, 1)
                return step

            def transposed_probs(m):
                n = sum(NT - s for s in PT_OF[m]) * P
                def step(i, b):
                    act.wait_ge(Z.full, Z.filled(i, f"b_pt{m}"))
                    nc.scalar.copy(pt_hi[:, m, 0:n], view(Z, i, f"b_pt{m}")[:, 0:n]).then_inc(pt_hi_done, 1)
                return step

            def b_pv(i, b):
                act.wait_ge(ctx_done, upto(ctx_done, b, 1))
                nc.scalar.copy(ctx_hi[:], ctxt[:]).then_inc(ctx_hi_done, 1)

            def b_o(i, b):
                act.wait_ge(Z.full, Z.filled(i, "b_o"))
                nc.scalar.activation(attn[:], view(Z, i, "b_o")[:], ACT.Identity,
                                     bias=cols[:, C_O:C_O + 1]).then_inc(attn_done, 1)

            def routed_up(name, k):
                def step(i, b):
                    act.wait_ge(Z.full, Z.filled(i, name))
                    act.wait_ge(hid16_done, upto(hid16_done, b, k - 1))
                    nc.scalar.activation(relu16[k % 2], view(Z, i, name)[:], ACT.Relu).then_inc(relu16_done, 1)
                return step

            def c_fin(i, b):
                act.wait_ge(pair_down, upto(pair_down, b, E // 2))
                nc.scalar.activation(g1, y1[:], ACT.Silu).then_inc(g1_done, 1)

            STEPS = {"a_xt": a_xt, "a_gt": a_gt, "r_up": r_up, "b_prob": b_prob, "r_exp": r_exp, "a_exp": a_exp,
                     "r_root": r_root, "b_hhi0": round_shared(0), "b_hhi1": round_shared(1), "b_silu": b_silu, "b_xt": b_xt,
                     "b_qsum": b_qsum, "b_ksum": b_ksum, "b_v": b_v, "b_route": b_route, "b_su0": shared_up(0),
                     "b_su1": shared_up(1), "b_sq0": squared(0), "b_sq1": squared(1), "b_gt": b_gt, "b_pt0": transposed_probs(0), "b_pt1": transposed_probs(1),
                     "b_pt2": transposed_probs(2), "b_pv": b_pv, "b_o": b_o, "c_fin": c_fin}
            for p in range(E // 2):
                for k, name in enumerate(PAIR[p]):
                    STEPS[name] = routed_up(name, 3 * p + k)

            def silu_of(i, h):
                act.wait_ge(G.full, G.filled(i, ("up", h)))
                act.wait_ge(mul_done, upto(mul_done, i, h - 1))
                nc.scalar.activation(silu[:, h % 2], view(G, i, ("up", h))[:], ACT.Silu).then_inc(silu_done, 1)

            def round_hid(i, h):
                if h < 2:
                    act.wait_ge(mul_done, upto(mul_done, i, h + 1))
                else:
                    act.wait_ge(gated_done, upto(gated_done, i, h - 1))
                act.wait_ge(down_done, upto(down_done, i, h - SLOTS + 1))
                r = slot(i, h)
                nc.scalar.copy(hid_hi[:, r], hid[:, h % WHOLE]).then_inc(hi_done, 1)

            def run(i):
                for h in range(NH):
                    if i.has("m"):
                        silu_of(i, h)
                    for part in range(3):
                        before = hidden_before(i, h, 1)
                        if part == ROUND_PART and before[0].has("m"):
                            round_hid(*before)
                        for s in steps("act", i, h, part):
                            STEPS[s](i, i.batch(s))

            def round_weights(c):
                act.wait_ge(w_in[c], 16)
                lo, hi = W_BOUNDS[c:c + 2]
                nc.scalar.copy(w_hi[:, lo:hi], w_stage[c][:, 0:hi - lo]).then_inc(w_rounded, 1)

            for c in range(2, W_CHUNKS):
                STEPS[f"w_s{c}"] = lambda i, b, c=c: round_weights(c)

            round_weights(0)
            a_xt(At(-1), At(0))
            round_weights(1)
            a_exp(At(-1), At(0))
            act.wait_ge(soft_dve, 1)
            nc.scalar.activation(decay[:, 1:2], decay[:, 0:1], ACT.Exp, scale=-1.0).then_inc(soft_act, 1)
            act.wait_ge(soft_act, 1)
            nc.scalar.activation(decay[:, 2:3], decay[:, 1:2], ACT.Ln, bias=1.0).then_inc(soft_act, 1)
            a_gt(At(-1), At(0))
            act.wait_ge(half_set, 2)
            iterations(act, run)

        @block.vector
        def _(dve):
            def statistics(b, src, stats, mv, var, stats_done, mv_done, var_done, rstd_done, dst_done):
                for n in range(NT):
                    nc.vector.bn_stats(stats[:, n, :], src[:, n, :]).then_inc(stats_done, 1)
                dve.wait_ge(dst_done, upto(dst_done, b, 0))
                dve.wait_ge(stats_done, upto(stats_done, b, NT))
                dve.sem_inc(passed_dve, 1)
                for n in range(NT):
                    nc.vector.bn_aggr(mv[:, n, :], stats[:, n, :]).then_inc(mv_done, 1)
                dve.wait_ge(mv_done, upto(mv_done, b, NT))
                dve.wait_ge(rstd_done, upto(rstd_done, b, 0))
                nc.vector.tensor_scalar_add(var[:], mv[:, :, 1], EPS).then_inc(var_done, 1)

            def normalise(b, src, mv, rstd, dst, rstd_done, dst_done):
                dve.wait_ge(rstd_done, upto(rstd_done, b, 1))
                for n in range(NT):
                    nc.vector.tensor_scalar(dst[:, n, :], src[:, n, :], mv[:, n, 0:1], rstd[:, n:n + 1],
                                            ALU.subtract, ALU.mult).then_inc(dst_done, 1)

            def wide(a, axis):
                return a.unsqueeze(axis).to_broadcast([P, NT, E, E])

            def ranks(b, s, values, beats, rank, k):
                nc.vector.tensor_tensor(beats[:], wide(values, 2), wide(values, 3), ALU.subtract).then_inc(s, 1)
                dve.wait_ge(s, upto(s, b, k + 1))
                nc.vector.tensor_tensor(beats[:], beats[:], ties[:].unsqueeze(1).to_broadcast([P, NT, E, E]),
                                        ALU.is_gt).then_inc(s, 1)
                dve.wait_ge(s, upto(s, b, k + 2))
                nc.vector.reduce_sum(rank[:], beats[:], axis=AX.X).then_inc(s, 1)
                dve.wait_ge(s, upto(s, b, k + 3))

            def a_norm(i, b):
                half = b.parity
                dve.wait_ge(x_loaded[half], upto(x_loaded[half], b, 16 - 8 * half))
                statistics(b, x_in[:, half], stats0, mv0, var0, stats0_done, mv0_done, var0_done, rstd0_done, xn0_done)

            def a_xn(i, b):
                dve.wait_ge(x0t_done, upto(x0t_done, b, 0))
                dve.wait_ge(x1t_done, upto(x1t_done, b + -2, 1))
                normalise(b, x_in[:, b.parity], mv0, rstd0, xn0, rstd0_done, xn0_done)

            def a_logits(i, b):
                z = view(U, i, "a_logits")[:, 0:NT * E].rearrange("p (n e) -> p n e", e=E)
                dve.wait_ge(U.full, U.filled(i, "a_logits"))
                nc.vector.reduce_max(top[:, :, 0], z, axis=AX.X).then_inc(router0, 1)
                dve.wait_ge(router0, upto(router0, b, 1))
                nc.vector.tensor_tensor(logit[:], z, top[:, :, 0:1].to_broadcast([P, NT, E]),
                                        ALU.subtract).then_inc(router0, 1)

            def a_gate(i, b):
                dve.wait_ge(exp0_done, upto(exp0_done, b, 1))
                nc.vector.reduce_sum(top[:, :, 1], score0[:], axis=AX.X).then_inc(router0, 1)
                dve.wait_ge(router0, upto(router0, b, 3))
                nc.vector.reciprocal(top[:, :, 2], top[:, :, 1]).then_inc(router0, 1)
                dve.wait_ge(router0, upto(router0, b, 4))
                nc.vector.tensor_tensor(score0[:], score0[:], top[:, :, 2:3].to_broadcast([P, NT, E]),
                                        ALU.mult).then_inc(router0, 1)
                dve.wait_ge(router0, upto(router0, b, 5))
                ranks(b, router0, score0[:], beats, rank, 5)
                nc.vector.scalar_tensor_tensor(score0[:], rank[:], 2.0, score0[:], ALU.is_lt,
                                               ALU.mult).then_inc(router0, 1)
                dve.wait_ge(router0, upto(router0, b, 9))
                nc.vector.reduce_sum(top[:, :, 1], score0[:], axis=AX.X).then_inc(router0, 1)
                dve.wait_ge(router0, upto(router0, b, 10))
                nc.vector.tensor_scalar_add(top[:, :, 3], top[:, :, 1], 1e-20).then_inc(router0, 1)
                dve.wait_ge(router0, upto(router0, b, 11))
                nc.vector.reciprocal(top[:, :, 2], top[:, :, 3]).then_inc(router0, 1)
                dve.wait_ge(router0, upto(router0, b, 12))
                dve.wait_ge(gate0_t_done, upto(gate0_t_done, b, 0))
                nc.vector.tensor_tensor(gate0[:], score0[:], top[:, :, 2:3].to_broadcast([P, NT, E]),
                                        ALU.mult).then_inc(router0, 1)

            def r_scan(i, b):
                dve.wait_ge(tanh_done, upto(tanh_done, b, 2))
                dve.wait_ge(a2_done, upto(a2_done, b, 0))
                nc.vector.tensor_scalar(log_a[:], tanh_a[:], 1.0, decay[:, 5:6], ALU.add, ALU.mult).then_inc(log_a_done, 1)
                dve.wait_ge(log_a_done, upto(log_a_done, b, 1))
                dve.wait_ge(normed_done, upto(normed_done, b, 0))
                nc.vector.memset(level[:, 0:1], 0.0).then_inc(level_done, 1)
                nc.vector.tensor_tensor_scan(level[:, 1:T], log_a[:, 0:T - 1],
                                             ln_floor[:].to_broadcast([P, T - 1]), 0.0,
                                             ALU.add, ALU.max).then_inc(level_done, 1)
                dve.wait_ge(level_done, upto(level_done, b, 2))
                dve.wait_ge(state_done, upto(state_done, b, 0))
                nc.vector.tensor_tensor(step_a[:, 1:T], level[:, 1:T], level[:, 0:T - 1],
                                        ALU.subtract).then_inc(step_done, 1)
                nc.vector.memset(step_a[:, 0:1], 0.0).then_inc(step_done, 1)
                dve.wait_ge(x0t_done, upto(x0t_done, b, 1))
                nc.vector.scalar_tensor_tensor(normed[:], tanh_x[:], 1.0, x0t[:], ALU.add, ALU.mult).then_inc(gated_x_done, 1)

            def r_room(i, b):
                dve.wait_ge(a2_done, upto(a2_done, b, 1))
                nc.vector.tensor_scalar(sq[:], sq[:], -1.0, -FLOOR, ALU.add, ALU.min).then_inc(room_done, 1)

            def r_fin(i, b):
                dve.wait_ge(root_done, upto(root_done, b, 1))
                nc.vector.tensor_tensor(normed[:], normed[:], sq[:], ALU.mult).then_inc(normed_done, 1)
                dve.wait_ge(normed_done, upto(normed_done, b, 1))
                dve.wait_ge(ratio_done, upto(ratio_done, b, 1))
                dve.wait_ge(sg0_done, upto(sg0_done, b, 0))
                nc.vector.tensor_tensor_scan(state[:], step_a[:], normed[:], 0.0, ALU.mult, ALU.add).then_inc(state_done, 1)

            def b_silu(i, b):
                dve.wait_ge(g0_done, upto(g0_done, b, 1))
                dve.wait_ge(state_done, upto(state_done, b, 1))
                dve.wait_ge(x1_done, upto(x1_done, b, 0))
                nc.vector.tensor_tensor(sg0[:], state[:], g0[:], ALU.mult).then_inc(sg0_done, 1)

            def b_tsg(i, b):
                dve.wait_ge(y_stored, upto(y_stored, b + -1, 0))
                dve.wait_ge(G.full, G.filled(i, "b_tsg"))
                g = view(G, i, "b_tsg")[:].rearrange("p (n d) -> p n d", d=P)
                nc.vector.tensor_tensor(x1[:, b.parity], x_in[:, b.parity], g, ALU.add).then_inc(x1_done, 1)
                dve.wait_ge(x1_done, upto(x1_done, b, 1))
                statistics(b, x1[:, b.parity], stats1, mv1, var1, stats1_done, mv1_done, var1_done, rstd1_done, xn1_done)

            def b_xn(i, b):
                dve.wait_ge(x1t_done, upto(x1t_done, b, 0))
                dve.wait_ge(x0t_done, upto(x0t_done, b, 2 if i.has("m") else 1))
                normalise(b, x1[:, b.parity], mv1, rstd1, xn1, rstd1_done, xn1_done)

            def rotated(name, k, column):
                def step(i, b):
                    dve.wait_ge(Z.full, Z.filled(i, name))
                    if k % 2 == 0:
                        dve.wait_ge(qk_lo_done, upto(qk_lo_done, b, 0))
                    nc.vector.scalar_tensor_tensor(rot[:, k], view(Z, i, name)[:], cols[:, column:column + 1],
                                                   cos_sin[:, k % 2], ALU.add, ALU.mult).then_inc(rot_done, 1)
                return step

            def b_v(i, b):
                dve.wait_ge(v_hi_done, upto(v_hi_done, b, 1))
                nc.vector.tensor_tensor(v_lo[:], view(Z, i, "b_v")[:], v_hi[:].bitcast(F32), ALU.subtract).then_inc(v_lo_done, 1)

            def b_ksum(i, b):
                dve.wait_ge(tanh1_done, upto(tanh1_done, b, 1))
                nc.vector.tensor_scalar(score1[:], tanh1[:], 0.5, 0.5, ALU.mult, ALU.add).then_inc(router1, 1)
                dve.wait_ge(router1, upto(router1, b, 1))
                nc.vector.tensor_tensor(biased[:], score1[:], bias8[:].unsqueeze(1).to_broadcast([P, NT, E]),
                                        ALU.add).then_inc(router1, 1)
                dve.wait_ge(router1, upto(router1, b, 2))
                ranks(b, router1, biased[:], beats1, rank1, 2)
                dve.wait_ge(gate1_t_done, upto(gate1_t_done, b, 0))
                nc.vector.scalar_tensor_tensor(gate1[:], rank1[:], 2.0, score1[:], ALU.is_lt,
                                               ALU.mult).then_inc(router1, 1)

            def mask_and_max(i, b, t, k):
                o = score_bank(i, t)
                nc.vector.tensor_tensor(o[:, tok(t)], o[:, tok(t)], causal, ALU.add).then_inc(masked_done, 1)
                dve.wait_ge(masked_done, upto(masked_done, b, k + 1))
                nc.vector.reduce_max(smax[:, t:t + 1], o, axis=AX.X).then_inc(max_done, 1)

            def b_s02(i, b):
                dve.wait_ge(Z.full, Z.filled(i, "b_s02"))
                mask_and_max(i, b, 0, 0)
                mask_and_max(i, b, 2, 1)

            def b_s3(i, b):
                dve.wait_ge(Z.full, Z.filled(i, "b_s3"))
                mask_and_max(i, b, 3, 2)

            def b_s1(i, b):
                dve.wait_ge(s1_full, upto(s1_full, b, 1))
                mask_and_max(i, b, 1, 3)
                dve.wait_ge(max_done, upto(max_done, b, NT))
                nc.vector.tensor_scalar_mul(nmax, smax, -SCALE).then_inc(nmax_done, 1)

            def b_pn(i, b):
                dve.wait_ge(prob_done, upto(prob_done, b, NT))
                nc.vector.reciprocal(rsum, ssum).then_inc(rsum_done, 1)
                dve.wait_ge(rsum_done, upto(rsum_done, b, 1))
                for t in range(NT):
                    nc.vector.tensor_scalar_mul(prob[:, PROB[t]], prob[:, PROB[t]], rsum[:, t:t + 1]).then_inc(prob_normed, 1)

            def transposed_probs(m):
                n = sum(NT - s for s in PT_OF[m]) * P
                def step(i, b):
                    dve.wait_ge(pt_hi_done, upto(pt_hi_done, b, m + 1))
                    nc.vector.tensor_tensor(pt_lo[:, m, 0:n], view(Z, i, f"b_pt{m}")[:, 0:n],
                                            pt_hi[:, m, 0:n].bitcast(F32), ALU.subtract).then_inc(pt_lo_done, 1)
                return step

            def b_pv(i, b):
                dve.wait_ge(Z.full, Z.filled(i, "b_pv"))
                dve.wait_ge(ctx_lo_done, upto(ctx_lo_done, b, 0))
                nc.vector.tensor_scalar_add(ctxt[:], view(Z, i, "b_pv")[:], cols[:, C_V:C_V + 1]).then_inc(ctx_done, 1)

            def gated_inputs(p):
                def step(i, b):
                    if p == 0:
                        dve.wait_ge(x1t_done, upto(x1t_done, b, 1))
                    for e in (2 * p, 2 * p + 1):
                        dve.wait_ge(relu16_done, upto(relu16_done, b, 3 * (p - 1)))
                        dve.wait_ge(gates1_in[e % RING1], upto(gates1_in[e % RING1], b, 16 * (e // RING1 + 1)))
                        nc.vector.tensor_tensor(routed_in[:, e % 4], x1t[:, b.parity], gates1[:, e % RING1], ALU.mult).then_inc(routed_in_done, 1)
                return step

            def routed_up(name, k):
                def step(i, b):
                    dve.wait_ge(relu16_done, upto(relu16_done, b, k + 1))
                    dve.wait_ge(pair_down, upto(pair_down, b, k // 3 - 1))
                    nc.vector.tensor_tensor(hid16[k % 6], relu16[k % 2], relu16[k % 2], ALU.mult).then_inc(hid16_done, 1)
                return step

            def c_fin(i, b):
                dve.wait_ge(g1_done, upto(g1_done, b, 1))
                dve.wait_ge(attn_done, upto(attn_done, b, 1))
                nc.vector.tensor_tensor(sg1, attn[:], g1, ALU.mult).then_inc(sg1_done, 1)

            def c_out(i, b):
                dve.wait_ge(Z.full, Z.filled(i, "c_out"))
                z = view(Z, i, "c_out")[:].rearrange("p (n d) -> p n d", d=P)
                nc.vector.tensor_tensor(y_out[:, b.parity], x1[:, b.parity], z, ALU.add).then_inc(y_done, 1)

            STEPS = {"a_norm": a_norm, "a_xn": a_xn, "b_xn": b_xn, "a_logits": a_logits, "a_gate": a_gate, "r_scan": r_scan,
                     "r_room": r_room,
                     "r_fin": r_fin, "b_silu": b_silu, "b_tsg": b_tsg, "b_q": rotated("b_q", 0, C_Q),
                     "b_qs": rotated("b_qs", 1, C_QS), "b_k": rotated("b_k", 2, C_K), "b_ks": rotated("b_ks", 3, C_KS),
                     "b_v": b_v, "b_ksum": b_ksum, "b_s02": b_s02, "b_s3": b_s3, "b_s1": b_s1, "b_pn": b_pn,
                     "b_pt0": transposed_probs(0), "b_pt1": transposed_probs(1), "b_pt2": transposed_probs(2),
                     "b_pv": b_pv, "c_fin": c_fin, "c_out": c_out}
            for p in range(E // 2):
                STEPS["bbcc"[p] + f"_x{p}"] = gated_inputs(p)
                for k, name in enumerate(PAIR[p]):
                    STEPS[name] = routed_up(name, 3 * p + k)

            def multiply(i, h):
                dve.wait_ge(silu_done, upto(silu_done, i, h + 1))
                dve.wait_ge(U.full, U.filled(i, ("up", h)))
                before, k = hidden_before(i, h, WHOLE)
                if before.has("m"):
                    lo = lo_dve if k in LO_DVE else lo_pool
                    dve.wait_ge(lo, upto(lo, before, lo_count(k)))
                nc.vector.tensor_tensor(hid[:, h % WHOLE], silu[:, h % 2], view(U, i, ("up", h))[:], ALU.mult).then_inc(mul_done, 1)

            def rest_of_hid(i, h):
                dve.wait_ge(hi_done, upto(hi_done, i, h + 1))
                r = slot(i, h)
                nc.vector.tensor_tensor(hid_lo[:, r], hid[:, h % WHOLE], hid_hi[:, r].bitcast(F32), ALU.subtract).then_inc(lo_dve, 1)

            def run(i):
                for h in range(NH):
                    for part in range(3):
                        if i.has("m") and part == MULTIPLY_PART:
                            multiply(i, h)
                        before = hidden_before(i, h, 1)
                        if part == LO_PART_DVE and before[0].has("m") and before[1] in LO_DVE:
                            rest_of_hid(*before)
                        for s in steps("dve", i, h, part):
                            STEPS[s](i, i.batch(s))
                if i.has("w"):
                    dve.wait_ge(rope_in, 16)
                    dve.wait_ge(const_in, 16)

            nc.vector.memset(ln_floor[:], LN_FLOOR).then_inc(const_set, 1)
            nc.vector.memset(minus_half[:], -0.5).then_inc(const_set, 1)
            a_norm(At(-1), At(0))
            a_xn(At(-1), At(0))
            def rest_of_weights(c):
                dve.wait_ge(w_rounded, c + 1)
                lo, hi = W_BOUNDS[c:c + 2]
                nc.vector.tensor_tensor(w_lo[:, lo:hi], w_stage[c][:, 0:hi - lo], w_hi[:, lo:hi].bitcast(F32),
                                        ALU.subtract).then_inc(w_split, 1)

            for c in range(2, W_CHUNKS):
                STEPS[f"w_s{c}"] = lambda i, b, c=c: rest_of_weights(c)

            rest_of_weights(0)
            dve.wait_ge(cols_in, 16)
            nc.vector.scalar_tensor_tensor(decay[:, 0:1], cols[:, C_A:C_A + 1], -1.0, cols[:, C_A:C_A + 1],
                                           ALU.mult, ALU.max).then_inc(soft_dve, 1)
            nc.vector.tensor_scalar_mul(half_bias[:], cols[:, C_IG:C_AG + 1], 0.5).then_inc(half_set, 1)
            rest_of_weights(1)
            a_logits(At(-1), At(0))
            dve.wait_ge(ties_in, 16)
            dve.wait_ge(bias8_in, 16)
            a_gate(At(-1), At(0))
            dve.wait_ge(soft_act, 2)
            nc.vector.tensor_scalar_max(decay[:, 3:4], cols[:, C_A:C_A + 1], 0.0).then_inc(soft_dve, 1)
            dve.wait_ge(soft_dve, 2)
            nc.vector.tensor_tensor(decay[:, 4:5], decay[:, 3:4], decay[:, 2:3], ALU.add).then_inc(soft_dve, 1)
            dve.wait_ge(soft_dve, 3)
            nc.vector.tensor_scalar_mul(decay[:, 5:6], decay[:, 4:5], -4.0).then_inc(half_set, 1)
            dve.wait_ge(half_set, 2)
            dve.wait_ge(const_set, 2)
            iterations(dve, run)

        @block.gpsimd
        def _(pool):
            TT = nc.gpsimd.tensor_tensor

            def a_norm(i, b):
                pool.wait_ge(var0_done, upto(var0_done, b, 1))
                pool.wait_ge(xn0_done, upto(xn0_done, b, 0))
                TT(rstd0[:], var0[:], minus_half[:], ALU.pow).then_inc(rstd0_done, 1)

            def a_xt(i, b):
                pool.wait_ge(x0t_done, upto(x0t_done, b, 1))
                pool.wait_ge(x0_hi_done, upto(x0_hi_done, b, 1))
                TT(x0_lo[:, b.parity], x0t[:], x0_hi[:, b.parity].bitcast(F32), ALU.subtract).then_inc(x0_lo_done, 1)

            def b_tsg(i, b):
                pool.wait_ge(var1_done, upto(var1_done, b, 1))
                pool.wait_ge(xn1_done, upto(xn1_done, b, 0))
                TT(rstd1[:], var1[:], minus_half[:], ALU.pow).then_inc(rstd1_done, 1)

            def b_xt(i, b):
                pool.wait_ge(x1t_done, upto(x1t_done, b, 1))
                pool.wait_ge(x1_hi_done, upto(x1_hi_done, b, 1))
                TT(x1_lo[:], x1t[:, b.parity], x1_hi[:].bitcast(F32), ALU.subtract).then_inc(x1_lo_done, 1)

            def rotated_sum(k):
                def step(i, b):
                    pool.wait_ge(rot_done, upto(rot_done, b, 2 * k + 2))
                    TT(rot[:, 2 * k], rot[:, 2 * k], rot[:, 2 * k + 1], ALU.add).then_inc(qk_done, 1)
                return step

            def rotated_lo(k, hi, lo):
                def step(i, b):
                    pool.wait_ge(qk_hi_done, upto(qk_hi_done, b, k + 1))
                    TT(lo, rot[:, 2 * k], hi.bitcast(F32), ALU.subtract).then_inc(qk_lo_done, 1)
                return step

            def shared_lo(j):
                def step(i, b):
                    pool.wait_ge(hs_hi_done, upto(hs_hi_done, b, j + 1))
                    TT(hs_lo[j], hs[:, j], hs_hi[j].bitcast(F32), ALU.subtract).then_inc(hs_lo_done, 1)
                return step

            def b_pv(i, b):
                pool.wait_ge(ctx_hi_done, upto(ctx_hi_done, b, 1))
                TT(ctx_lo[:], ctxt[:], ctx_hi[:].bitcast(F32), ALU.subtract).then_inc(ctx_lo_done, 1)

            STEPS = {"a_norm": a_norm, "a_xt": a_xt, "b_tsg": b_tsg, "b_xt": b_xt,
                     "b_qsum": rotated_sum(0), "b_ksum": rotated_sum(1),
                     "b_qlo": rotated_lo(0, q_hi, q_lo), "b_klo": rotated_lo(1, k_hi, k_lo),
                     "b_hlo0": shared_lo(0), "b_hlo1": shared_lo(1),
                     "b_pv": b_pv}

            def gate(i, h):
                e = h // 2 - 1
                pool.wait_ge(gates0_in[e % RING0], upto(gates0_in[e % RING0], i, 16 * (e // RING0 + 1)))
                pool.wait_ge(mul_done, upto(mul_done, i, h + 1))
                r = h % WHOLE
                TT(hid[:, r], hid[:, r], gates0[:, e % RING0], ALU.mult).then_inc(gated_done, 1)

            def rest_of_hid(i, h):
                pool.wait_ge(hi_done, upto(hi_done, i, h + 1))
                r = slot(i, h)
                TT(hid_lo[:, r], hid[:, h % WHOLE], hid_hi[:, r].bitcast(F32), ALU.subtract).then_inc(lo_pool, 1)

            def run(i):
                for h in range(NH):
                    for part in range(3):
                        if i.has("m") and h >= 2 and part == GATE_PART:
                            gate(i, h)
                        before = hidden_before(i, h, 1)
                        if part == LO_PART_POOL and before[0].has("m") and before[1] not in LO_DVE:
                            rest_of_hid(*before)
                        for s in steps("pool", i, h, part):
                            STEPS[s](i, i.batch(s))

            pool.wait_ge(const_set, 2)
            a_norm(At(-1), At(0))
            a_xt(At(-1), At(0))

            def cast_weights(c):
                pool.wait_ge(w16_in[c], 16)
                nc.gpsimd.tensor_copy(w16[:, c * V_CHUNK:(c + 1) * V_CHUNK], w16_stage[c]).then_inc(w16_cast, 1)

            for c in range(V_CHUNKS):
                STEPS[f"w_c{c}"] = lambda i, b, c=c: cast_weights(c)

            iterations(pool, run)


def kernel(**inputs):
    import numpy as np
    import concourse.bacc as _bacc
    from concourse import mybir as _mybir
    from concourse.bass_utils import run_bass_kernel_spmd as _run

    a = {k: np.asarray(v) for k, v in inputs.items()}
    f32 = np.float32

    def block_diagonal(w):
        out = np.zeros((P, P), f32)
        n = w.shape[1]
        for h in range(w.shape[0]):
            out[h * n:(h + 1) * n, h * n:(h + 1) * n] = w[h]
        return out

    def swapped(w):
        return w.reshape(*w.shape[:-1], -1, 2)[..., ::-1].reshape(w.shape)

    up0 = [np.concatenate([a["L0_ffn_Sg"], a["L0_ffn_Su"]], 1)]
    up0 += [np.concatenate([a["L0_ffn_Wg"][e], a["L0_ffn_Wu"][e]], 1) for e in range(E)]
    down0 = [w.reshape(HID0 // P, P, P).transpose(1, 0, 2).reshape(P, HID0)
             for w in [a["L0_ffn_Sd"], *a["L0_ffn_Wd"]]]
    shared_up = np.zeros((P, 2 * P), f32)
    shared_up[:, :HID1] = a["L1_ffn_shared_w_up"].T
    shared_down = np.zeros((2 * P, P), f32)
    shared_down[:HID1] = a["L1_ffn_shared_w_down"].T
    shared_down = shared_down.reshape(2, P, P).transpose(1, 0, 2).reshape(P, 2 * P)
    experts0 = [w for pair in zip(up0, down0) for w in pair]
    weights = np.concatenate(
        [a["L0_ffn_Wr"], a["L1_ffn_gate_w"].T, block_diagonal(a["L0_attn_ig_w"]), block_diagonal(a["L0_attn_ag_w"]),
         *experts0, a["L1_attn_Wq"], swapped(a["L1_attn_Wq"]), a["L1_attn_Wk"], swapped(a["L1_attn_Wk"]),
         a["L1_attn_Wv"], a["L1_attn_Wo"], shared_up, shared_down], 1)

    w_up, w_down = a["L1_ffn_w_up"], a["L1_ffn_w_down"]
    rest_up = np.zeros((P, E, HALF), f32)
    rest_down = np.zeros((E, HALF, P), f32)
    for e in range(E):
        rest_up[:, e, :REM] = w_up[e, P:, :].T
        rest_down[e, :REM] = w_down[e, :, P:].T
    weights16 = np.concatenate(
        [w_up[:, :P, :].transpose(2, 0, 1).reshape(P, E * P), rest_up.reshape(P, E * HALF),
         w_down[:, :, :P].transpose(2, 0, 1).reshape(P, E * P),
         rest_down.reshape(E // 2, P, P).transpose(1, 0, 2).reshape(P, E // 2 * P)], 1)

    columns = np.stack(
        [a["L0_attn_ig_b"].reshape(P), a["L0_attn_ag_b"].reshape(P), a["L0_attn_a_param"], a["L1_attn_bq"],
         swapped(a["L1_attn_bq"]), a["L1_attn_bk"], swapped(a["L1_attn_bk"]), a["L1_attn_bv"], a["L1_attn_bo"]], 1)

    inv_freq = (f32(1.0) / f32(10000.0) ** (np.arange(0, P, 2, dtype=f32) / f32(P))).astype(f32)
    angles = np.repeat(np.arange(T, dtype=f32)[None, :] * inv_freq[:, None], 2, axis=0)
    sign = np.where(np.arange(P) % 2 == 0, -1.0, 1.0).astype(f32)[:, None]
    rope = np.stack([np.cos(angles), np.sin(angles) * sign], 1).astype(f32)
    masks = np.stack([np.eye(P, dtype=f32), np.triu(np.full((P, P), MASKED, f32), 1)], 1)
    n = np.arange(E)
    rank_ties = np.tile(np.where(n[None, :] < n[:, None], -1e-37, 0.0).astype(f32).reshape(1, E * E), (P, 1))

    nc = _bacc.Bacc("TRN2", target_bir_lowering=False, num_devices=1)
    arrays, args = {}, []
    for name, v in [("x", a["L0_attn_x"]), ("weights", weights), ("weights16", weights16), ("columns", columns),
                    ("rope", rope), ("masks", masks), ("rank_ties", rank_ties),
                    ("expert_bias", a["L1_ffn_expert_bias"])]:
        v = np.ascontiguousarray(v)
        arrays[name] = v
        args.append(nc.dram_tensor(name, v.shape, _mybir.dt.from_np(v.dtype), kind="ExternalInput").ap())
    args.append(nc.dram_tensor("out", (NB, T, P), _mybir.dt.float32, kind="ExternalOutput").ap())
    build_layers(nc, *args)
    return _run(nc, [arrays], core_ids=[0]).results[0]["out"]
```
